# Optimizing a Trainium2 kernel written in Bass

```python
import numpy as np
import jax
import jax.numpy as jnp

def _softmax(x, axis=-1):
    return jax.nn.softmax(x, axis=axis)
def _gelu(x):
    return jax.nn.gelu(x, approximate=True)
def _silu(x):
    return jax.nn.silu(x)
def _sigmoid(x):
    return jax.nn.sigmoid(x)
def _layernorm(x, axis=-1, eps=1e-5):
    m = jnp.mean(x, axis=axis, keepdims=True)
    v = jnp.var(x, axis=axis, keepdims=True)
    return (x - m) / jnp.sqrt(v + eps)
def _scatter_add(tgt, idx, src, axis=0):
    return tgt.at[idx].add(src)
def _segment_sum(src, seg, n):
    return jax.ops.segment_sum(src, seg, n)

kernel_name = 'mk_conv_preact_d1_conv_nchw256_e681e6'

def setup_inputs(seed: int = 0):
    np.random.seed(seed)
    _w = jnp.asarray
    def _rec_inputs():
        import jax
        import jax.numpy as jnp
        _gk = jax.random.key(seed)
        x = 1.508e-05 + 1 * jax.random.normal(jax.random.fold_in(_gk, 1), (4, 256, 256, 256), jnp.float32)
        return x
    x = _rec_inputs()
    def _L0_conv_setup():
        import jax, jax.numpy as jnp
        import numpy as np
        N = 4
        C = 256
        H = 256
        W = 256
        P = 32
        W_GRAD = 0.5
        W_ACT = 0.5
        PROP = 0.5

        def _grad_mag(x):
            n, c, h, w = x.shape
            xf = x.reshape(n * c, 1, h, w)
            gx = jnp.array([[[[-1.0, 0.0, 1.0]]]], dtype=x.dtype)
            gy = jnp.array([[[[-1.0], [0.0], [1.0]]]], dtype=x.dtype)
            dn = ('NCHW', 'OIHW', 'NCHW')
            ex = jax.lax.conv_general_dilated(xf, gx, (1, 1), ((0, 0), (1, 1)), dimension_numbers=dn)
            ey = jax.lax.conv_general_dilated(xf, gy, (1, 1), ((1, 1), (0, 0)), dimension_numbers=dn)
            return (jnp.abs(ex) + jnp.abs(ey)).reshape(n, c, h, w)
        key = jax.random.key(seed)
        x = jax.random.normal(key, (N, C, H, W), dtype=jnp.float32)
        return {'x': x}
    _L0_conv_all = _L0_conv_setup()
    _L0_conv_in = {k: v for k, v in _L0_conv_all.items() if k in ()}
    del _L0_conv_all

    return {
        "x": x,
    }

def reference(x):
    import jax
    import jax.numpy as jnp
    def _L0_conv_ref(x):
        import jax, jax.numpy as jnp
        import numpy as np
        N = 4
        C = 256
        H = 256
        W = 256
        P = 32
        W_GRAD = 0.5
        W_ACT = 0.5
        PROP = 0.5

        def _grad_mag(x):
            n, c, h, w = x.shape
            xf = x.reshape(n * c, 1, h, w)
            gx = jnp.array([[[[-1.0, 0.0, 1.0]]]], dtype=x.dtype)
            gy = jnp.array([[[[-1.0], [0.0], [1.0]]]], dtype=x.dtype)
            dn = ('NCHW', 'OIHW', 'NCHW')
            ex = jax.lax.conv_general_dilated(xf, gx, (1, 1), ((0, 0), (1, 1)), dimension_numbers=dn)
            ey = jax.lax.conv_general_dilated(xf, gy, (1, 1), ((1, 1), (0, 0)), dimension_numbers=dn)
            return (jnp.abs(ex) + jnp.abs(ey)).reshape(n, c, h, w)
        n = x.shape[0]
        nh, nw = (H // P, W // P)
        num_patches = nh * nw
        k = max(1, int(PROP * C))
        s = W_GRAD * _grad_mag(x) + W_ACT * jnp.abs(x)
        sp = s.reshape(n, C, nh, P, nw, P).mean(axis=(3, 5))
        sp = sp.reshape(n, C, num_patches)
        order = jnp.argsort(-sp, axis=1)
        ranks = jnp.argsort(order, axis=1)
        mask = (ranks < k).astype(x.dtype)
        mask_sp = mask.reshape(n, C, nh, nw)[:, :, :, None, :, None]
        out = (x.reshape(n, C, nh, P, nw, P) * mask_sp).reshape(n, C, H, W)
        return out

    def _gn(v, G=32, eps=1e-5):
        B_, C_, H_, W_ = v.shape
        g = v.reshape(B_, G, C_ // G, H_, W_)
        m = jnp.mean(g, axis=(2, 3, 4), keepdims=True)
        s = jnp.var(g, axis=(2, 3, 4), keepdims=True)
        return ((g - m) / jnp.sqrt(s + eps)).reshape(v.shape)

    def _ln_c(v, eps=1e-6):
        m = jnp.mean(v, axis=1, keepdims=True)
        s = jnp.var(v, axis=1, keepdims=True)
        return (v - m) / jnp.sqrt(s + eps)

    def _ln_t(v, eps=1e-5):
        m = jnp.mean(v, axis=-1, keepdims=True)
        s = jnp.var(v, axis=-1, keepdims=True)
        return (v - m) / jnp.sqrt(s + eps)

    def _to_tokens(v):
        B_, C_, H_, W_ = v.shape
        return v.reshape(B_, C_, H_ * W_).transpose(0, 2, 1)
    def _from_tokens(t, like):
        B_, C_, H_, W_ = like.shape
        return t.transpose(0, 2, 1).reshape(B_, C_, H_, W_)

    x = x + _L0_conv_ref(_gn(x))
    return x


_drawn_inputs = setup_inputs


def setup_inputs(seed=0):
    import zlib

    import numpy as np

    out = dict(_drawn_inputs(seed))
    spreads = {}
    factors = {}
    for name, (base, spread) in spreads.items():
        noise = np.random.default_rng([zlib.crc32(name.encode()), seed]).standard_normal(out[name].shape)
        drawn = base * np.exp(spread * noise) if base else spread * noise
        out[name] = jnp.asarray(drawn.astype(out[name].dtype))
    for name, factor in factors.items():
        out[name] = (out[name] * factor).astype(out[name].dtype)
    return out
```

```python
import concourse.bass as bass
from concourse import mybir
from contextlib import ExitStack

FP32 = mybir.dt.float32
BF16 = mybir.dt.bfloat16
ALU = mybir.AluOpType
ACT = mybir.ActivationFunctionType
AX = mybir.AxisListType

IMAGES, CHANNELS, HEIGHT, WIDTH = 4, 256, 256, 256
GROUPS = 32
PATCH = 32
KEPT = CHANNELS // 2
EPS = 1e-5

PARTS = 128
BANDS = HEIGHT // PATCH
COLS = WIDTH // PATCH
TILE_CH = PARTS // BANDS
TILES = CHANNELS // TILE_CH
PIX = PATCH * WIDTH
HALF = PIX // 2
GROUP_PARTS = CHANNELS // GROUPS * BANDS
PATCHES = BANDS * COLS

RING = 3
SLOTS = 3
LOOPED = (TILES - 1) // RING
LAST = TILES - 1
BN = 512
CHUNKS = PIX // BN

PE_PATCHES = 6
ITEMS = 5
ROUNDS = KEPT // 8
DIFF_ITEMS = [(0, 0, 0), (2, 1, PE_PATCHES), (1, 0, 2), (0, 0, 4), (1, 0, 6)]
DIFF_BEFORE = [-1, -3, 0, 1, 3]
ACT_ORDER = [("diff", 0), ("diff", 1), ("diff", 2), ("vertical", 0), ("diff", 3), ("diff", 4), ("diff", 5),
             ("vertical", 1), ("diff", 6), ("diff", 7), ("diff", 8), ("vertical", 2), ("diff", 9),
             ("centred", 0), ("centred", 1), ("vertical", 3), ("centred", 2), ("centred", 3), ("centred", 4),
             ("vertical", 4), ("centred", 5), ("centred", 6), ("vertical", 5), ("centred", 7)]

REC = 3 + COLS


def groupnorm_patch_topk(nc: bass.Bass, x: bass.AP, out: bass.AP):
    ctx = ExitStack()
    with ctx:
        def sb(name, shape, dt=FP32):
            return ctx.enter_context(nc.sbuf_tensor(name, shape, dt))

        def pb(name, shape, dt=FP32):
            return ctx.enter_context(nc.psum_tensor(name, shape, dt))

        def sem(name):
            return ctx.enter_context(nc.semaphore(name))

        ring = [sb(f"ring{b}", [PARTS, PIX]) for b in range(RING)]
        kept = sb("kept", [PARTS, PIX])
        again = [sb(f"again{b}", [PARTS, HALF]) for b in range(SLOTS)]
        diff = [sb(f"diff{b}", [PARTS, PATCH, 2 * PATCH]) for b in range(3)]

        plus = sb("plus", [PARTS, PARTS])
        minus = sb("minus", [PARTS, PARTS])
        from_above = sb("from_above", [PARTS, PARTS])
        from_below = sb("from_below", [PARTS, PARTS])
        at_top = sb("at_top", [PARTS, PARTS])
        at_bottom = sb("at_bottom", [PARTS, PARTS])
        averager = sb("averager", [PARTS, PARTS])
        same_channel = sb("same_channel", [PARTS, TILE_CH])
        same_band = sb("same_band", [PARTS, BANDS])
        same_band16 = sb("same_band16", [PARTS, BANDS], BF16)
        scale = sb("scale", [PARTS, TILES])
        minus_half = sb("minus_half", [PARTS, TILES])

        stats = sb("stats", [PARTS, CHUNKS, 6])
        record = [sb(f"record{b}", [PARTS, REC]) for b in range(RING + 1)]
        sums = [sb(f"sums{b}", [PARTS, 3, COLS]) for b in range(RING + 1)]
        records = sb("records", [PARTS, TILES, REC])
        spread = sb("spread", [PARTS, TILES])
        spread2 = sb("spread2", [PARTS, TILES])
        var = sb("var", [PARTS, TILES])
        rstd = sb("rstd", [PARTS, TILES])
        newton = sb("newton", [PARTS, TILES])
        scores = sb("scores", [PARTS, TILES, COLS])
        largest = sb("largest", [PATCHES, 8])
        coef = sb("coef", [PARTS, TILES, 2, COLS])
        coef_now = sb("coef_now", [PARTS, 2, COLS])

        vertical = [pb(f"vertical{b}", [PARTS, PATCH, PATCH]) for b in range(2)]
        small_bank = pb("small_bank", [PARTS, 512])
        halo_bank = small_bank[:, 0:4 * PATCH].rearrange("p (a w) -> p a w", a=2)
        mean_bank = small_bank[:, 256:512]
        rank_bank = pb("rank_bank", [PARTS, 512])
        score_bank = rank_bank[:, 0:CHANNELS]
        mask_bank = rank_bank[:, CHANNELS:CHANNELS + TILES * COLS]
        junk = pb("junk", [PARTS, PATCH, PATCH])
        idle = diff[2][:].rearrange("p r w -> p (r w)")
        spread_cols = TILES * PATCHES
        by_band = idle[:, 0:spread_cols].rearrange("p (t b w) -> p t b w", b=BANDS, w=COLS)
        chosen = idle[0:PATCHES, spread_cols:].bitcast(BF16).rearrange("p (c b) -> p c b", b=BANDS)
        left = diff[1][0:PATCHES].rearrange("p r w -> p (r w)")[:, 0:CHANNELS]

        constants = sem("constants")
        ring_loaded = [sem(f"ring_loaded{b}") for b in range(RING)]
        kept_loaded = sem("kept_loaded")
        again_loaded = [sem(f"again_loaded{b}") for b in range(SLOTS)]
        again_stored = [sem(f"again_stored{b}") for b in range(SLOTS)]
        kept_stored = sem("kept_stored")
        stats_ready = sem("stats_ready")
        mean_ready = sem("mean_ready")
        minus_mean_ready = sem("minus_mean_ready")
        halo_ready = sem("halo_ready")
        halo_free = sem("halo_free")
        diff_ready = sem("diff_ready")
        diff_free = sem("diff_free")
        vertical_ready = sem("vertical_ready")
        vertical_free = sem("vertical_free")
        centred = sem("centred")
        recorded = sem("recorded")
        spread_ready = sem("spread_ready")
        var_ready = sem("var_ready")
        stable_var_ready = sem("stable_var_ready")
        rstd_ready = sem("rstd_ready")
        by_band_ready = sem("by_band_ready")
        gathered = sem("gathered")
        chosen_ready = sem("chosen_ready")
        mask_ready = sem("mask_ready")
        applied = sem("applied")

        finished = sem("finished")
        buffers = [kept, *ring]
        order = [LAST, *range(LAST - RING, LAST)]
        finished_stored = [sem(f"finished_stored{b}") for b in range(len(buffers))]
        refilled = [sem(f"refilled{b}") for b in range(len(buffers))]

        block = ctx.enter_context(nc.Block())

        CONSTANTS = 21
        PER_IMAGE = 2 * TILES
        CREDIT_DIFF, CREDIT_VERTICAL, CREDIT_HALO, CREDIT_RECORDED = ITEMS, 2, 1, 2
        CREDIT_CENTRED = 1
        CREDIT_STORED = 16
        ANALYSED = COLS

        @block.gpsimd
        def _(pool):
            steps = [0]

            def make(ins):
                steps[0] += 1
                ins.then_inc(constants, 1)
                pool.wait_ge(constants, steps[0])

            def diagonal(columns, count, step, base, value):
                make(nc.gpsimd.affine_select(out=columns, in_=columns, compare_op=ALU.not_equal, fill=value,
                                             base=base, pattern=[[-step, count]], channel_multiplier=1))

            def bands(m, band):
                return m[:].rearrange("p (c b) -> p c b", b=BANDS)[:, :, band]

            pool.sem_inc(diff_free, CREDIT_DIFF)
            pool.sem_inc(vertical_free, CREDIT_VERTICAL)
            pool.sem_inc(halo_free, CREDIT_HALO)
            pool.sem_inc(recorded, CREDIT_RECORDED)
            pool.sem_inc(centred, CREDIT_CENTRED)
            for stored in again_stored:
                pool.sem_inc(stored, CREDIT_STORED)
            make(nc.gpsimd.memset(minus_half[:], -0.5))
            make(nc.gpsimd.memset(same_channel[:], 1.0))
            make(nc.gpsimd.memset(averager[:], 0.0))
            make(nc.gpsimd.memset(plus[:], 0.0))
            for m in (minus, from_above, from_below, at_top, at_bottom):
                make(nc.gpsimd.memset(m[:], 0.0))
            for first in range(0, PARTS, GROUP_PARTS):
                make(nc.gpsimd.memset(averager[first:first + GROUP_PARTS, first:first + GROUP_PARTS],
                                      1.0 / GROUP_PARTS))
            diagonal(plus[:], PARTS, 1, 0, 1.0)
            diagonal(minus[:], PARTS, 1, 0, -1.0)
            diagonal(bands(at_top, 0), TILE_CH, BANDS, 0, 1.0)
            diagonal(bands(at_bottom, BANDS - 1), TILE_CH, BANDS, 1 - BANDS, 1.0)
            diagonal(from_above[:], PARTS, 1, 1, -1.0)
            diagonal(from_below[:], PARTS, 1, -1, -1.0)
            make(nc.gpsimd.memset(bands(from_above, 0), 0.0))
            make(nc.gpsimd.memset(bands(from_below, BANDS - 1), 0.0))
            make(nc.gpsimd.affine_select(out=same_channel[:], in_=same_channel[:], compare_op=ALU.is_ge, fill=0.0,
                                         base=0, pattern=[[-BANDS, TILE_CH]], channel_multiplier=1))
            make(nc.gpsimd.affine_select(out=same_channel[:], in_=same_channel[:], compare_op=ALU.is_ge, fill=0.0,
                                         base=BANDS - 1, pattern=[[BANDS, TILE_CH]], channel_multiplier=-1))
            assert steps[0] == CONSTANTS

            with pool.Fori(0, IMAGES) as image:
                pool.wait_ge(stable_var_ready, image + 1)
                nc.gpsimd.tensor_tensor(rstd[:], var[:], minus_half[:], ALU.pow).then_inc(rstd_ready, 1)

        @block.sync
        def _(sp):
            def load_tile(tile, buffer, signal):
                sp.dma_start(buffer[:], x[bass.ds(tile, 1)].rearrange("a p f -> p (a f)")).then_inc(signal, 16)

            def load_half(tile, half, slot):
                sp.dma_start(again[slot][:], x[bass.ds(tile, 1), :, half * HALF:(half + 1) * HALF]
                             .rearrange("a p f -> p (a f)")).then_inc(again_loaded[slot], 16)

            def store_tile(tile, buffer, signal):
                sp.dma_start(out[bass.ds(tile, 1)].rearrange("a p f -> p (a f)"), buffer[:]).then_inc(signal, 16)

            def store_half(tile, half, source, signal):
                sp.dma_start(out[bass.ds(tile, 1), :, half * HALF:(half + 1) * HALF]
                             .rearrange("a p f -> p (a f)"), source).then_inc(signal, 16)

            def load_two_ahead(image, g, u):
                tile = TILES * image + RING * g + u
                sp.wait_ge(centred, ANALYSED * tile + CREDIT_CENTRED)
                load_tile(tile + 2, ring[(u + 2) % RING], ring_loaded[(u + 2) % RING])

            def load_again(image, g, q):
                sp.wait_ge(again_stored[q % SLOTS],
                           16 * (2 * LOOPED * image - 2 * LOOPED + 2 * g + q // SLOTS) + CREDIT_STORED)
                load_half(TILES * image - TILES + RING * g + q // 2, q % 2, q % SLOTS)

            def finish_tile(image, g, u):
                for h in range(2):
                    q = 2 * u + h
                    sp.wait_ge(applied, PER_IMAGE * image - PER_IMAGE + 2 * RING * g + q + 3)
                    store_half(TILES * image - TILES + RING * g + u, h, again[q % SLOTS][:],
                               again_stored[q % SLOTS])
                    if q + 2 < 2 * RING or not (isinstance(g, int) and g == LOOPED - 1):
                        load_again(image, g, q + 2)

            load_tile(0, ring[0], ring_loaded[0])
            load_tile(1, ring[1], ring_loaded[1])
            load_tile(2, ring[2], ring_loaded[2])
            load_two_ahead(0, 0, 1)
            load_two_ahead(0, 0, 2)
            with sp.Fori(1, LOOPED - 1) as g:
                for u in range(RING):
                    load_two_ahead(0, g, u)
            load_two_ahead(0, LOOPED - 1, 0)
            load_tile(LAST, kept, kept_loaded)

            with sp.Fori(1, IMAGES) as image:
                sp.wait_ge(centred, ANALYSED * (TILES * image - 3) + CREDIT_CENTRED)
                load_tile(TILES * image, ring[0], ring_loaded[0])
                sp.wait_ge(centred, ANALYSED * (TILES * image - 2) + CREDIT_CENTRED)
                load_tile(TILES * image + 1, ring[1], ring_loaded[1])
                load_again(image, 0, 0)
                load_again(image, 0, 1)
                load_two_ahead(image, 0, 0)
                for h in range(2):
                    sp.wait_ge(applied, PER_IMAGE * image - PER_IMAGE + h + 1)
                    store_half(TILES * image - 1, h, kept[:, h * HALF:(h + 1) * HALF], kept_stored)
                finish_tile(image, 0, 0)
                for u in range(1, RING):
                    load_two_ahead(image, 0, u)
                    finish_tile(image, 0, u)
                with sp.Fori(1, LOOPED - 1) as g:
                    for u in range(RING):
                        load_two_ahead(image, g, u)
                        finish_tile(image, g, u)
                load_two_ahead(image, LOOPED - 1, 0)
                finish_tile(image, LOOPED - 1, 0)
                sp.wait_ge(kept_stored, 32 * image)
                load_tile(TILES * image + LAST, kept, kept_loaded)
                finish_tile(image, LOOPED - 1, 1)
                finish_tile(image, LOOPED - 1, 2)

            base = TILES * (IMAGES - 1)
            resident = TILES - len(buffers)

            def finish(n):
                b = n % len(buffers)
                tile = base + (order[n] if isinstance(n, int) and n < len(buffers) else n - len(buffers))
                sp.wait_ge(finished, n + 1)
                store_tile(tile, buffers[b], finished_stored[b])

            def refill(i, b, stores):
                sp.wait_ge(finished_stored[b], 16 * stores)
                load_tile(base + i, buffers[b], refilled[b])

            finish(0)
            for n in range(1, len(buffers)):
                finish(n)
                refill(n - 1, n - 1, 1)
            with sp.Fori(0, resident // len(buffers) - 1) as k:
                for b in range(len(buffers)):
                    before = (b - 1) % len(buffers)
                    i = len(buffers) * k + b + len(buffers) - 1
                    sp.wait_ge(finished_stored[before], 16 * (k + (2 if before < b else 1)))
                    load_tile(base + i, buffers[before], refilled[before])
                    sp.wait_ge(finished, len(buffers) * k + len(buffers) + b + 1)
                    store_tile(base + len(buffers) * k + b, buffers[b], finished_stored[b])
            rounds = resident // len(buffers)
            refill(resident - 1, len(buffers) - 1, rounds)
            for n in range(TILES - len(buffers), TILES):
                sp.wait_ge(finished, n + 1)
                store_tile(base + n - len(buffers), buffers[n % len(buffers)], finished_stored[n % len(buffers)])
            for b in range(len(buffers)):
                sp.wait_ge(finished_stored[b], 16 * (rounds + 1))
            for slot in range(SLOTS):
                sp.wait_ge(again_stored[slot], 16 * 2 * LOOPED * (IMAGES - 1) + CREDIT_STORED)
            sp.wait_ge(kept_stored, 32 * (IMAGES - 1))

        @block.tensor
        def _(pe):
            def mean(tile, r):
                pe.wait_ge(stats_ready, tile + 1)
                nc.tensor.matmul(mean_bank[:, 0:1], averager[:], record[r][:, 0:1], start=True, stop=True)\
                    .then_inc(mean_ready, 1)

            def border(target, matrix, halo, edge, minus_mean, accumulate):
                n = halo.shape[1]
                nc.tensor.matmul(target, matrix[:], halo, start=not accumulate, stop=False)
                return nc.tensor.matmul(target, edge[:], minus_mean.broadcast_to([PARTS, n]), start=False, stop=True)

            def differences(tile, buffer, r, before_last):
                rows = buffer[:].rearrange("p (r w) -> p r w", w=WIDTH)
                minus_mean = record[r][:, 2:3]
                pe.wait_ge(minus_mean_ready, tile + 1)
                pe.wait_ge(halo_free, tile + CREDIT_HALO)
                first = PE_PATCHES * PATCH
                border(halo_bank[:, 0, 0:WIDTH - first], from_above, rows[:, PATCH - 1, first:], at_top,
                       minus_mean, False)
                border(halo_bank[:, 1, 0:WIDTH - first], from_below, rows[:, 0, first:], at_bottom,
                       minus_mean, False).then_inc(halo_ready, 1)
                mid = PATCH // 2
                for w in range(PE_PATCHES):
                    if w == PE_PATCHES - 1:
                        before_last()
                    c = slice(w * PATCH, (w + 1) * PATCH)
                    v = vertical[w % 2]
                    pe.wait_ge(vertical_free, PE_PATCHES * tile + w - 1 + CREDIT_VERTICAL)
                    nc.tensor.matmul(v[:, 0:mid, :], plus[:], rows[:, 1:mid + 1, c], start=True, stop=False)
                    nc.tensor.matmul(v[:, 1:mid, :], minus[:], rows[:, 0:mid - 1, c], start=False, stop=False)
                    border(v[:, 0, :], from_above, rows[:, PATCH - 1, c], at_top, minus_mean, True)
                    nc.tensor.matmul(v[:, mid:PATCH, :], plus[:], rows[:, mid - 1:PATCH - 1, c],
                                     start=True, stop=False)
                    nc.tensor.matmul(v[:, mid:PATCH - 1, :], minus[:], rows[:, mid + 1:PATCH, c],
                                     start=False, stop=False)
                    border(v[:, PATCH - 1, :], from_below, rows[:, 0, c], at_bottom, minus_mean, True)\
                        .then_inc(vertical_ready, 1)

            def image_tiles(image):
                with pe.Fori(0, LOOPED - 1) as g:
                    for u in range(RING):
                        tile = TILES * image + RING * g + u
                        differences(tile, ring[u], u, lambda: mean(tile + 1, (u + 1) % RING))
                for u in range(RING):
                    tile = TILES * image + LAST - RING + u
                    differences(tile, ring[u], u, lambda: mean(tile + 1, u + 1))
                differences(TILES * image + LAST, kept, RING, lambda: None)

            def rank(image):
                pe.wait_ge(spread_ready, image + 1)
                nc.tensor.matmul(mean_bank[:, 16:16 + TILES], averager[:], spread[:], start=True, stop=True)\
                    .then_inc(var_ready, 1)
                pe.wait_ge(by_band_ready, image + 1)
                for t in range(TILES):
                    moved = nc.tensor.matmul(score_bank[0:PATCHES, t * TILE_CH:(t + 1) * TILE_CH],
                                             by_band[:, t].rearrange("p b w -> p (b w)"), same_channel[:],
                                             start=True, stop=True)
                moved.then_inc(gathered, 1)
                pe.wait_ge(chosen_ready, image + 1)
                for t in range(TILES):
                    moved = nc.tensor.matmul(mask_bank[:, t * COLS:(t + 1) * COLS],
                                             chosen[:, t * TILE_CH:(t + 1) * TILE_CH, :]
                                             .rearrange("p c b -> p (c b)"),
                                             same_band16[0:PATCHES, :], start=True, stop=True)
                moved.then_inc(mask_ready, 1)

            pe.wait_ge(constants, CONSTANTS)
            mean(0, 0)
            image_tiles(0)
            with pe.Fori(1, IMAGES) as image:
                mean(TILES * image, 0)
                rank(image - 1)
                image_tiles(image)
            rank(IMAGES - 1)

        @block.scalar
        def _(act):
            def sums_of(tile, buffer, r):
                rows = buffer[:].rearrange("p (r w) -> p r w", w=WIDTH)
                act.wait_ge(recorded, tile - 1 + CREDIT_RECORDED)
                for kind, n in ACT_ORDER:
                    if kind == "diff":
                        item, side = divmod(n, 2)
                        slot, which, w = DIFF_ITEMS[item]
                        if side == 0:
                            act.wait_ge(diff_ready, ITEMS * tile + item + 1)
                        v = diff[slot][:, :, side * PATCH:(side + 1) * PATCH]
                        w += side
                        done = nc.scalar.activation(v, v, ACT.Abs, accum_out=sums[r][:, which, w:w + 1])
                        if side == 1:
                            done.then_inc(diff_free, 1)
                    elif kind == "vertical":
                        act.wait_ge(vertical_ready, PE_PATCHES * tile + n + 1)
                        v = vertical[n % 2][:]
                        done = nc.scalar.activation(v, v, ACT.Abs, accum_out=sums[r][:, 1, n:n + 1])
                        done.then_inc(vertical_free, 1)
                    else:
                        if n == 0:
                            act.wait_ge(minus_mean_ready, tile + 1)
                        act.wait_ge(centred, COLS * tile + n + CREDIT_CENTRED)
                        done = nc.scalar.activation(junk[:], rows[:, :, n * PATCH:(n + 1) * PATCH], ACT.Abs,
                                                    bias=record[r][:, 2:3], accum_out=sums[r][:, 2, n:n + 1])
                        done.then_inc(centred, 1)


            act.wait_ge(constants, CONSTANTS)
            with act.Fori(0, IMAGES) as image:
                with act.Fori(0, LOOPED) as g:
                    for u in range(RING):
                        sums_of(TILES * image + RING * g + u, ring[u], u)
                sums_of(TILES * image + LAST, kept, RING)

        @block.vector
        def _(dve):
            def settle():
                dve.drain()

            def statistics(tile, buffer, r, loaded, count):
                dve.wait_ge(loaded, 16 * count)
                for k in range(CHUNKS):
                    nc.vector.bn_stats(stats[:, k, :], buffer[:, k * BN:(k + 1) * BN])
                settle()
                nc.vector.bn_aggr(record[r][:, 0:2], stats[:]).then_inc(stats_ready, 1)

            def minus_mean(tile, r):
                dve.wait_ge(mean_ready, tile + 1)
                nc.vector.tensor_scalar(record[r][:, 2:3], mean_bank[:, 0:1], -1.0, None, ALU.mult)\
                    .then_inc(minus_mean_ready, 1)

            def differences(tile, buffer, r):
                settle()
                rows = buffer[:].rearrange("p (r w) -> p r w", w=WIDTH)
                nm = record[r][:, 2:3]
                wide = 2 * PATCH
                for item, (slot, which, w) in enumerate(DIFF_ITEMS):
                    d = diff[slot]
                    left_col = w * PATCH
                    dve.wait_ge(diff_free, ITEMS * tile + DIFF_BEFORE[item] + CREDIT_DIFF)
                    if which == 0:
                        lo = 1 if w == 0 else 0
                        hi = wide - 1 if w == COLS - 2 else wide
                        if w == 0:
                            nc.vector.tensor_scalar(d[:, :, 0:1], rows[:, :, 1:2], nm, None, ALU.add)
                        if w == COLS - 2:
                            nc.vector.tensor_scalar(d[:, :, hi:], rows[:, :, WIDTH - 2:WIDTH - 1], nm, None, ALU.add)
                        nc.vector.tensor_tensor(d[:, :, lo:hi], rows[:, :, left_col + lo + 1:left_col + hi + 1],
                                                rows[:, :, left_col + lo - 1:left_col + hi - 1], ALU.subtract)\
                            .then_inc(diff_ready, 1)
                    else:
                        c = slice(left_col, left_col + wide)
                        dve.wait_ge(halo_ready, tile + 1)
                        nc.vector.tensor_tensor(d[:, 0, :], rows[:, 1, c], halo_bank[:, 0, 0:wide], ALU.add)
                        nc.vector.tensor_tensor(d[:, PATCH - 1, :], rows[:, PATCH - 2, c], halo_bank[:, 1, 0:wide],
                                                ALU.add).then_inc(halo_free, 1)
                        nc.vector.tensor_tensor(d[:, 1:PATCH - 1, :], rows[:, 2:PATCH, c], rows[:, 0:PATCH - 2, c],
                                                ALU.subtract).then_inc(diff_ready, 1)

            def read_sums(tile, r):
                dve.wait_ge(centred, ANALYSED * (tile + 1) + CREDIT_CENTRED)
                nc.vector.tensor_reduce(record[r][:, 3:REC], sums[r][:].rearrange("p k w -> p w k"), AX.X, ALU.add)

            def keep_record(r, t):
                nc.vector.tensor_scalar(records[:, bass.ds(t, 1), :].rearrange("p a k -> p (a k)"), record[r][:],
                                        1.0, None, ALU.mult).then_inc(recorded, 1)

            def fetch_coefficients(t):
                nc.vector.tensor_scalar(coef_now[:].rearrange("p a w -> p (a w)"),
                                        coef[:, bass.ds(t, 1)].rearrange("p t a w -> p (t a w)"),
                                        1.0, None, ALU.mult)

            def apply(pixels, signal):
                rows = pixels.rearrange("p (r w) -> p r w", w=WIDTH)
                for w in range(COLS):
                    v = rows[:, :, w * PATCH:(w + 1) * PATCH]
                    done = nc.vector.tensor_scalar(v, v, coef_now[:, 0, w:w + 1], coef_now[:, 1, w:w + 1],
                                                   ALU.mult, ALU.add)
                done.then_inc(signal, 1)

            def apply_again(image, g, q):
                dve.wait_ge(again_loaded[q % SLOTS],
                            16 * (2 * LOOPED * image - 2 * LOOPED + 2 * g + q // SLOTS + 1))
                apply(again[q % SLOTS][:], applied)

            def step(image, g, u, before, after, count, output):
                tile = TILES * image + RING * g + u
                differences(tile, ring[u], u)
                if before is not None:
                    read_sums(tile - 1, before)
                if output:
                    fetch_coefficients(RING * g + u)
                settle()
                if before is not None:
                    keep_record(before, RING * g + u - 1)
                if output:
                    apply_again(image, g, 2 * u)
                statistics(tile + 1, places[after], after, place_loaded[after], count)
                if output:
                    apply_again(image, g, 2 * u + 1)
                minus_mean(tile + 1, after)

            def image_tiles(image, output):
                loads = LOOPED * image
                step(image, 0, 0, None, 1, loads + 1, output)
                step(image, 0, 1, 0, 2, loads + 1, output)
                step(image, 0, 2, 1, 0, loads + 2, output)
                with dve.Fori(1, LOOPED - 1) as g:
                    for u in range(RING):
                        step(image, g, u, (u - 1) % RING, (u + 1) % RING, loads + g + (u + 1) // RING + 1, output)
                step(image, LOOPED - 1, 0, RING - 1, 1, loads + LOOPED, output)
                step(image, LOOPED - 1, 1, 0, 2, loads + LOOPED, output)
                step(image, LOOPED - 1, 2, 1, RING, image + 1, output)
                tile = TILES * image + LAST
                differences(tile, kept, RING)
                read_sums(tile - 1, RING - 1)
                settle()
                keep_record(RING - 1, LAST - 1)

            def rank(image):
                read_sums(TILES * image + LAST, RING)
                settle()
                keep_record(RING, LAST)
                settle()
                part_mean, part_var, nm = (records[:, :, k] for k in range(3))
                nc.vector.tensor_tensor(spread2[:], part_mean, nm, ALU.add)
                settle()
                nc.vector.tensor_tensor(newton[:], spread2[:], spread2[:], ALU.mult)
                settle()
                nc.vector.tensor_tensor(spread[:], newton[:], part_var, ALU.add).then_inc(spread_ready, 1)
                dve.wait_ge(var_ready, image + 1)
                nc.vector.tensor_scalar(var[:], mean_bank[:, 16:16 + TILES], EPS, None, ALU.add)\
                    .then_inc(stable_var_ready, 1)
                dve.wait_ge(rstd_ready, image + 1)
                nc.vector.tensor_tensor(newton[:], rstd[:], rstd[:], ALU.mult)
                settle()
                nc.vector.tensor_tensor(spread2[:], newton[:], var[:], ALU.mult)
                settle()
                nc.vector.tensor_scalar(newton[:], spread2[:], -0.5, 1.5, ALU.mult, ALU.add)
                settle()
                nc.vector.tensor_tensor(scale[:], rstd[:], newton[:], ALU.mult)
                settle()
                scale3 = scale[:].unsqueeze(2).broadcast_to([PARTS, TILES, COLS])
                nc.vector.tensor_tensor(scores[:], records[:, :, 3:REC], scale3, ALU.mult)
                settle()
                nc.vector.tensor_tensor(by_band,
                                        scores[:].unsqueeze(2).broadcast_to([PARTS, TILES, BANDS, COLS]),
                                        same_band[:].unsqueeze(1).unsqueeze(3)
                                        .broadcast_to([PARTS, TILES, BANDS, COLS]),
                                        ALU.mult).then_inc(by_band_ready, 1)
                dve.wait_ge(gathered, image + 1)
                nc.vector.tensor_copy(left, score_bank[0:PATCHES, :])
                settle()
                with dve.Fori(0, ROUNDS):
                    nc.vector.max(largest[:], left)
                    settle()
                    nc.vector.match_replace(out=left, in_to_replace=largest[:], in_values=left, imm_value=-1.0)
                    settle()
                nc.vector.scalar_tensor_tensor(out=chosen,
                                               in0=left.unsqueeze(2).broadcast_to([PATCHES, CHANNELS, BANDS]),
                                               scalar=0.0,
                                               in1=same_channel[0:PATCHES, 0:BANDS].unsqueeze(1)
                                               .broadcast_to([PATCHES, CHANNELS, BANDS]),
                                               op0=ALU.is_lt, op1=ALU.mult).then_inc(chosen_ready, 1)
                dve.wait_ge(mask_ready, image + 1)
                nc.vector.tensor_tensor(scores[:],
                                        mask_bank.rearrange("p (t w) -> p t w", w=COLS),
                                        scale3, ALU.mult)
                settle()
                nc.vector.tensor_scalar(coef[:, :, 0, :], scores[:], 1.0, None, ALU.add)
                nc.vector.tensor_tensor(coef[:, :, 1, :], scores[:],
                                        nm.unsqueeze(2).broadcast_to([PARTS, TILES, COLS]), ALU.mult)
                settle()

            places = [*ring, kept]
            place_loaded = [*ring_loaded, kept_loaded]

            dve.wait_ge(constants, CONSTANTS)
            nc.vector.tensor_reduce(same_band[:], plus[:].rearrange("p (c b) -> p b c", b=BANDS), AX.X, ALU.add)
            settle()
            nc.vector.tensor_copy(same_band16[:], same_band[:])

            statistics(0, ring[0], 0, ring_loaded[0], 1)
            minus_mean(0, 0)
            image_tiles(0, False)
            with dve.Fori(1, IMAGES) as image:
                statistics(TILES * image, ring[0], 0, ring_loaded[0], LOOPED * image + 1)
                minus_mean(TILES * image, 0)
                rank(image - 1)
                fetch_coefficients(LAST)
                settle()
                apply(kept[:, 0:HALF], applied)
                apply(kept[:, HALF:PIX], applied)
                image_tiles(image, True)
            rank(IMAGES - 1)

            for n, t in enumerate(order):
                settle()
                fetch_coefficients(t)
                settle()
                apply(buffers[n][:], finished)
            with dve.Fori(0, (TILES - len(buffers)) // len(buffers)) as k:
                for b in range(len(buffers)):
                    settle()
                    fetch_coefficients(len(buffers) * k + b)
                    settle()
                    dve.wait_ge(refilled[b], 16 * (k + 1))
                    apply(buffers[b][:], finished)


def kernel(**inputs):
    import numpy as _np
    import concourse.bacc as _bacc
    from concourse import mybir as _mybir
    from concourse.bass_utils import run_bass_kernel_spmd as _run

    nc = _bacc.Bacc("TRN2", target_bir_lowering=False, num_devices=1)
    a = _np.ascontiguousarray(inputs["x"])
    shape = a.shape
    a = a.reshape(IMAGES * TILES, PARTS, PIX)
    x = nc.dram_tensor("in_x_dram", a.shape, _mybir.dt.from_np(a.dtype), kind="ExternalInput").ap()
    out = nc.dram_tensor("out_0_dram", a.shape, _mybir.dt.from_np(a.dtype), kind="ExternalOutput").ap()
    groupnorm_patch_topk(nc, x, out)
    r = _run(nc, [{"in_x_dram": a}], core_ids=[0])
    return r.results[0]["out_0_dram"].reshape(shape)
```

```python
import concourse.bass as bass
from concourse import mybir
from contextlib import ExitStack

FP32 = mybir.dt.float32
BF16 = mybir.dt.bfloat16
ALU = mybir.AluOpType
ACT = mybir.ActivationFunctionType
AX = mybir.AxisListType

IMAGES, CHANNELS, HEIGHT, WIDTH = 4, 256, 256, 256
GROUPS = 32
PATCH = 32
KEPT = CHANNELS // 2
EPS = 1e-5

PARTS = 128
BANDS = HEIGHT // PATCH
COLS = WIDTH // PATCH
TILE_CH = PARTS // BANDS
TILES = CHANNELS // TILE_CH
PIX = PATCH * WIDTH
HALF = PIX // 2
GROUP_PARTS = CHANNELS // GROUPS * BANDS
PATCHES = BANDS * COLS

RING = 3
SLOTS = 3
LOOPED = (TILES - 1) // RING
LAST = TILES - 1
BN = 512
CHUNKS = PIX // BN

PE_PATCHES = 6
ITEMS = 5
ROUNDS = KEPT // 8
ROUNDS_UNROLLED = 4
VERTICAL_ITEM = 2
DIFF_ITEMS = [(0, 0, 0), (1, 0, 2), (2, 1, PE_PATCHES), (0, 0, 4), (1, 0, 6)]
EARLY_ITEMS = 2
DIFF_BEFORE = [-1, 0, -2, 1, 2]
ACT_ORDER = [("diff", 0), ("diff", 1), ("vertical", 0), ("diff", 2), ("diff", 3), ("centred", 0),
             ("vertical", 1), ("centred", 1), ("centred", 2), ("centred", 3), ("vertical", 2),
             ("centred", 4), ("centred", 5), ("centred", 6), ("vertical", 3), ("diff", 4), ("diff", 5),
             ("diff", 6), ("diff", 7), ("vertical", 4), ("diff", 8), ("diff", 9), ("vertical", 5), ("centred", 7)]
ACT_LAST_DIFF = ("diff", 2 * ITEMS - 1)
ACT_ORDER_FIRST = [(kind, n) for kind, n in ACT_ORDER if kind != "diff" or n < 2 * ITEMS - 2]


REC = 3 + COLS


def groupnorm_patch_topk(nc: bass.Bass, x: bass.AP, out: bass.AP):
    ctx = ExitStack()
    with ctx:
        def sb(name, shape, dt=FP32):
            return ctx.enter_context(nc.sbuf_tensor(name, shape, dt))

        def pb(name, shape, dt=FP32):
            return ctx.enter_context(nc.psum_tensor(name, shape, dt))

        def sem(name):
            return ctx.enter_context(nc.semaphore(name))

        ring = [sb(f"ring{b}", [PARTS, PIX]) for b in range(RING)]
        kept = sb("kept", [PARTS, PIX])
        again = [sb(f"again{b}", [PARTS, HALF]) for b in range(SLOTS)]
        diff = [sb(f"diff{b}", [PARTS, PATCH, 2 * PATCH]) for b in range(3)]

        plus = sb("plus", [PARTS, PARTS])
        minus = sb("minus", [PARTS, PARTS])
        from_above = sb("from_above", [PARTS, PARTS])
        from_below = sb("from_below", [PARTS, PARTS])
        at_top = sb("at_top", [PARTS, PARTS])
        at_bottom = sb("at_bottom", [PARTS, PARTS])
        averager = sb("averager", [PARTS, PARTS])
        same_channel = sb("same_channel", [PARTS, TILE_CH])
        same_band = sb("same_band", [PARTS, BANDS])
        same_band16 = sb("same_band16", [PARTS, BANDS], BF16)
        scale = sb("scale", [PARTS, TILES])
        minus_half = sb("minus_half", [PARTS, TILES])

        stats = sb("stats", [PARTS, CHUNKS, 6])
        record = [sb(f"record{b}", [PARTS, REC]) for b in range(RING + 1)]
        sums = [sb(f"sums{b}", [PARTS, 3, COLS]) for b in range(RING + 1)]
        records = sb("records", [PARTS, TILES, REC])
        spread = sb("spread", [PARTS, TILES])
        spread2 = sb("spread2", [PARTS, TILES])
        var = sb("var", [PARTS, TILES])
        rstd = sb("rstd", [PARTS, TILES])
        newton = sb("newton", [PARTS, TILES])
        scores = sb("scores", [PARTS, TILES, COLS])
        largest = sb("largest", [PATCHES, 8])
        coef = sb("coef", [PARTS, TILES, 2, COLS])
        coef_now = sb("coef_now", [PARTS, 2, COLS])

        vertical = [pb(f"vertical{b}", [PARTS, PATCH, PATCH]) for b in range(2)]
        small_bank = pb("small_bank", [PARTS, 512])
        halo_bank = small_bank[:, 0:4 * PATCH].rearrange("p (a w) -> p a w", a=2)
        mean_bank = small_bank[:, 256:512]
        rank_bank = pb("rank_bank", [PARTS, 512])
        score_bank = rank_bank[:, 0:CHANNELS]
        mask_bank = rank_bank[:, CHANNELS:CHANNELS + TILES * COLS]
        var_bank = rank_bank[:, CHANNELS + TILES * COLS:CHANNELS + TILES * COLS + TILES]
        junk = pb("junk", [PARTS, PATCH, PATCH])
        idle = diff[2][:].rearrange("p r w -> p (r w)")
        spread_cols = TILES * PATCHES
        by_band = idle[:, 0:spread_cols].rearrange("p (t b w) -> p t b w", b=BANDS, w=COLS)
        chosen = idle[0:PATCHES, spread_cols:].bitcast(BF16).rearrange("p (c b) -> p c b", b=BANDS)
        left = coef[0:PATCHES].rearrange("p t a w -> p (t a w)")

        constants = sem("constants")
        first_loaded = [sem(f"first_loaded{k}") for k in range(4)]
        ring_loaded = [sem(f"ring_loaded{b}") for b in range(RING)]
        kept_loaded = sem("kept_loaded")
        again_loaded = [sem(f"again_loaded{b}") for b in range(SLOTS)]
        again_stored = [sem(f"again_stored{b}") for b in range(SLOTS)]
        kept_stored = sem("kept_stored")
        stats_ready = sem("stats_ready")
        mean_ready = sem("mean_ready")
        minus_mean_ready = sem("minus_mean_ready")
        halo_ready = sem("halo_ready")
        halo_free = sem("halo_free")
        diff_ready = sem("diff_ready")
        diff_free = sem("diff_free")
        vertical_ready = sem("vertical_ready")
        vertical_free = sem("vertical_free")
        analysed = sem("analysed")
        centred = sem("centred")
        recorded = sem("recorded")
        spread_ready = sem("spread_ready")
        var_ready = sem("var_ready")
        stable_var_ready = sem("stable_var_ready")
        rstd_ready = sem("rstd_ready")
        by_band_ready = sem("by_band_ready")
        gathered = sem("gathered")
        chosen_ready = sem("chosen_ready")
        mask_ready = sem("mask_ready")
        applied = sem("applied")

        finished = sem("finished")
        buffers = [kept, *ring]
        BUFFERS = len(buffers)
        REFILLS = TILES - BUFFERS - 1
        order = [LAST, *range(LAST - RING, LAST)]
        finished_stored = [sem(f"finished_stored{b}") for b in range(len(buffers))]
        refilled = [sem(f"refilled{b}") for b in range(len(buffers))]

        block = ctx.enter_context(nc.Block())

        CONSTANTS = 21
        PER_IMAGE = 2 * TILES
        CREDIT_DIFF, CREDIT_VERTICAL, CREDIT_HALO, CREDIT_RECORDED = ITEMS, 2, 1, 2
        CREDIT_STORED = 16

        @block.gpsimd
        def _(pool):
            steps = [0]

            def make(ins):
                steps[0] += 1
                ins.then_inc(constants, 1)
                pool.wait_ge(constants, steps[0])

            def diagonal(columns, count, step, base, value):
                make(nc.gpsimd.affine_select(out=columns, in_=columns, compare_op=ALU.not_equal, fill=value,
                                             base=base, pattern=[[-step, count]], channel_multiplier=1))

            def bands(m, band):
                return m[:].rearrange("p (c b) -> p c b", b=BANDS)[:, :, band]

            pool.sem_inc(diff_free, CREDIT_DIFF)
            pool.sem_inc(vertical_free, CREDIT_VERTICAL)
            pool.sem_inc(halo_free, CREDIT_HALO)
            pool.sem_inc(recorded, CREDIT_RECORDED)
            for stored in (*again_stored, kept_stored):
                pool.sem_inc(stored, CREDIT_STORED)
            make(nc.gpsimd.memset(minus_half[:], -0.5))
            make(nc.gpsimd.memset(same_channel[:], 1.0))
            make(nc.gpsimd.memset(averager[:], 0.0))
            make(nc.gpsimd.memset(plus[:], 0.0))
            for m in (minus, from_above, from_below, at_top, at_bottom):
                make(nc.gpsimd.memset(m[:], 0.0))
            for first in range(0, PARTS, GROUP_PARTS):
                make(nc.gpsimd.memset(averager[first:first + GROUP_PARTS, first:first + GROUP_PARTS],
                                      1.0 / GROUP_PARTS))
            diagonal(plus[:], PARTS, 1, 0, 1.0)
            diagonal(minus[:], PARTS, 1, 0, -1.0)
            diagonal(bands(at_top, 0), TILE_CH, BANDS, 0, 1.0)
            diagonal(bands(at_bottom, BANDS - 1), TILE_CH, BANDS, 1 - BANDS, 1.0)
            diagonal(from_above[:], PARTS, 1, 1, -1.0)
            diagonal(from_below[:], PARTS, 1, -1, -1.0)
            make(nc.gpsimd.memset(bands(from_above, 0), 0.0))
            make(nc.gpsimd.memset(bands(from_below, BANDS - 1), 0.0))
            make(nc.gpsimd.affine_select(out=same_channel[:], in_=same_channel[:], compare_op=ALU.is_ge, fill=0.0,
                                         base=0, pattern=[[-BANDS, TILE_CH]], channel_multiplier=1))
            make(nc.gpsimd.affine_select(out=same_channel[:], in_=same_channel[:], compare_op=ALU.is_ge, fill=0.0,
                                         base=BANDS - 1, pattern=[[BANDS, TILE_CH]], channel_multiplier=-1))
            assert steps[0] == CONSTANTS

            with pool.Fori(0, IMAGES) as image:
                pool.wait_ge(stable_var_ready, image + 1)
                nc.gpsimd.tensor_tensor(rstd[:], var[:], minus_half[:], ALU.pow).then_inc(rstd_ready, 1)

        @block.sync
        def _(sp):
            def load_tile(tile, buffer, signal):
                sp.dma_start(buffer[:], x[bass.ds(tile, 1)].rearrange("a p f -> p (a f)")).then_inc(signal, 16)

            def load_half(tile, half, slot):
                sp.dma_start(again[slot][:], x[bass.ds(tile, 1), :, half * HALF:(half + 1) * HALF]
                             .rearrange("a p f -> p (a f)")).then_inc(again_loaded[slot], 16)

            def store_tile(tile, buffer, signal):
                sp.dma_start(out[bass.ds(tile, 1)].rearrange("a p f -> p (a f)"), buffer[:]).then_inc(signal, 16)

            def store_half(tile, half, source, signal):
                sp.dma_start(out[bass.ds(tile, 1), :, half * HALF:(half + 1) * HALF]
                             .rearrange("a p f -> p (a f)"), source).then_inc(signal, 16)

            def load_two_ahead(image, g, u, last=False):
                tile = TILES * image + RING * g + u
                if isinstance(g, int) and RING * g + u == LAST - 2:
                    sp.wait_ge(kept_stored, 32 * image + CREDIT_STORED)
                    load_tile(tile + 2, kept, kept_loaded)
                elif isinstance(g, int) and RING * g + u > LAST - 2:
                    b = RING * g + u - LAST + 1
                    if not last:
                        sp.wait_ge(analysed, tile - 1)
                        load_tile(tile + 2, ring[b], ring_loaded[b])
                else:
                    sp.wait_ge(analysed, tile)
                    load_tile(tile + 2, ring[(u + 2) % RING], ring_loaded[(u + 2) % RING])

            def load_again(image, g, w):
                sp.wait_ge(again_stored[w % SLOTS],
                           16 * (2 * LOOPED * image - 2 * LOOPED + 2 * g + w // SLOTS) + CREDIT_STORED)
                load_half(TILES * image - TILES + RING * g + w // 2, w % 2, w % SLOTS)

            def finish_before(image, g, u):
                for h in range(2):
                    w = 2 * u - 2 + h
                    sp.wait_ge(applied, PER_IMAGE * image - PER_IMAGE + 2 * RING * g + w + 3)
                    store_half(TILES * image - TILES + RING * g + u - 1, h, again[w % SLOTS][:],
                               again_stored[w % SLOTS])
                    if not (isinstance(g, int) and 2 * RING * g + w + 2 >= 2 * LAST):
                        load_again(image, g, w + 2)

            def image_loads(image, last):
                load_two_ahead(image, 0, 0)
                load_again(image, 0, 0)
                load_again(image, 0, 1)
                for h in range(2):
                    sp.wait_ge(applied, PER_IMAGE * image - PER_IMAGE + h + 1)
                    store_half(TILES * image - 1, h, kept[:, h * HALF:(h + 1) * HALF], kept_stored)
                for u in range(1, RING):
                    load_two_ahead(image, 0, u)
                    finish_before(image, 0, u)
                with sp.Fori(1, LOOPED - 1) as g:
                    for u in range(RING):
                        load_two_ahead(image, g, u)
                        finish_before(image, g, u)
                for u in range(RING + 1):
                    load_two_ahead(image, LOOPED - 1, u, last)
                    finish_before(image, LOOPED - 1, u)

            for quarter, loaded in enumerate(first_loaded):
                part = slice(quarter * PIX // 4, (quarter + 1) * PIX // 4)
                sp.dma_start(ring[0][:, part], x[0, :, part]).then_inc(loaded, 16)
            load_tile(1, ring[1], ring_loaded[1])
            load_tile(2, ring[2], ring_loaded[2])
            load_two_ahead(0, 0, 1)
            load_two_ahead(0, 0, 2)
            with sp.Fori(1, LOOPED - 1) as g:
                for u in range(RING):
                    load_two_ahead(0, g, u)
            for u in range(RING + 1):
                load_two_ahead(0, LOOPED - 1, u)
            with sp.Fori(1, IMAGES - 1) as image:
                image_loads(image, False)
            image_loads(IMAGES - 1, True)

            load_again(IMAGES, 0, 0)
            load_again(IMAGES, 0, 1)
            base = TILES * (IMAGES - 1)

            def refill(tile, b, stores):
                sp.wait_ge(finished_stored[b], 16 * stores)
                load_tile(base + tile, buffers[b], refilled[b])

            def finish(tile, b, count):
                sp.wait_ge(finished, count)
                store_tile(base + tile, buffers[b], finished_stored[b])

            finish(order[0], 0, 1)
            for n in range(1, BUFFERS):
                finish(order[n], n, n + 1)
                refill(n, n - 1, 1)
            for h in range(2):
                sp.wait_ge(finished, BUFFERS + h + 1)
                store_half(base, h, again[h][:], again_stored[h])
            counted = BUFFERS + 2
            with sp.Fori(0, REFILLS // BUFFERS) as k:
                for b in range(BUFFERS):
                    before = (b - 1) % BUFFERS
                    finish(BUFFERS * k + b + 1, b, BUFFERS * k + b + 1 + counted)
                    refill(BUFFERS * k + b + BUFFERS, before, k + (2 if before < b else 1))
            done = REFILLS // BUFFERS * BUFFERS
            for n in range(done, REFILLS):
                finish(n + 1, n % BUFFERS, n + 1 + counted)
            for b in range(BUFFERS):
                sp.wait_ge(finished_stored[b], 16 * (1 + len(range(b, REFILLS, BUFFERS))))
            for slot in range(SLOTS):
                sp.wait_ge(again_stored[slot],
                           16 * (2 * LOOPED * (IMAGES - 1) + (slot < 2)) + CREDIT_STORED)
            sp.wait_ge(kept_stored, 32 * (IMAGES - 1) + CREDIT_STORED)

        @block.tensor
        def _(pe):
            def mean(tile, r):
                pe.wait_ge(stats_ready, tile + 1)
                nc.tensor.matmul(mean_bank[:, 0:1], averager[:], record[r][:, 0:1], start=True, stop=True)\
                    .then_inc(mean_ready, 1)

            def border(target, matrix, halo, edge, minus_mean, accumulate):
                n = halo.shape[1]
                nc.tensor.matmul(target, matrix[:], halo, start=not accumulate, stop=False)
                return nc.tensor.matmul(target, edge[:], minus_mean.broadcast_to([PARTS, n]), start=False, stop=True)

            def halo(tile, buffer, r):
                rows = buffer[:].rearrange("p (r w) -> p r w", w=WIDTH)
                pe.wait_ge(minus_mean_ready, tile + 1)
                pe.wait_ge(halo_free, tile + CREDIT_HALO)
                first = PE_PATCHES * PATCH
                border(halo_bank[:, 0, 0:WIDTH - first], from_above, rows[:, PATCH - 1, first:], at_top,
                       record[r][:, 2:3], False)
                border(halo_bank[:, 1, 0:WIDTH - first], from_below, rows[:, 0, first:], at_bottom,
                       record[r][:, 2:3], False).then_inc(halo_ready, 1)

            def differences(tile, buffer, r, patches):
                rows = buffer[:].rearrange("p (r w) -> p r w", w=WIDTH)
                minus_mean = record[r][:, 2:3]
                mid = PATCH // 2
                for w in patches:
                    c = slice(w * PATCH, (w + 1) * PATCH)
                    v = vertical[w % 2]
                    pe.wait_ge(vertical_free, PE_PATCHES * tile + w - 1 + CREDIT_VERTICAL)
                    nc.tensor.matmul(v[:, 0:mid, :], plus[:], rows[:, 1:mid + 1, c], start=True, stop=False)
                    nc.tensor.matmul(v[:, 1:mid, :], minus[:], rows[:, 0:mid - 1, c], start=False, stop=False)
                    border(v[:, 0, :], from_above, rows[:, PATCH - 1, c], at_top, minus_mean, True)
                    nc.tensor.matmul(v[:, mid:PATCH, :], plus[:], rows[:, mid - 1:PATCH - 1, c],
                                     start=True, stop=False)
                    nc.tensor.matmul(v[:, mid:PATCH - 1, :], minus[:], rows[:, mid + 1:PATCH, c],
                                     start=False, stop=False)
                    border(v[:, PATCH - 1, :], from_below, rows[:, 0, c], at_bottom, minus_mean, True)\
                        .then_inc(vertical_ready, 1)

            def tile_work(tile, buffer, r, after):
                halo(tile, buffer, r)
                differences(tile, buffer, r, range(PE_PATCHES))
                if after is not None:
                    mean(tile + 1, after)

            def first_tile(image):
                tile = TILES * image
                ranking = not isinstance(image, int)
                if ranking:
                    variances(image - 1)
                mean(tile, 0)
                halo(tile, ring[0], 0)
                differences(tile, ring[0], 0, range(0, 2))
                if ranking:
                    gather(image - 1)
                differences(tile, ring[0], 0, range(2, 4))
                if ranking:
                    mask(image - 1)
                differences(tile, ring[0], 0, range(4, PE_PATCHES))
                mean(tile + 1, 1)

            def image_tiles(image):
                first_tile(image)
                tile_work(TILES * image + 1, ring[1], 1, 2)
                tile_work(TILES * image + 2, ring[2], 2, 0)
                with pe.Fori(1, LOOPED - 1) as g:
                    for u in range(RING):
                        tile_work(TILES * image + RING * g + u, ring[u], u, (u + 1) % RING)
                for u in range(RING):
                    tile_work(TILES * image + LAST - RING + u, ring[u], u, u + 1)
                tile_work(TILES * image + LAST, kept, RING, None)

            def variances(image):
                pe.wait_ge(spread_ready, image + 1)
                nc.tensor.matmul(var_bank, averager[:], spread[:], start=True, stop=True).then_inc(var_ready, 1)

            def gather(image):
                for count, tiles in ((1, range(LAST)), (2, [LAST])):
                    pe.wait_ge(by_band_ready, 2 * image + count)
                    for t in tiles:
                        moved = nc.tensor.matmul(score_bank[0:PATCHES, t * TILE_CH:(t + 1) * TILE_CH],
                                                 by_band[:, t].rearrange("p b w -> p (b w)"), same_channel[:],
                                                 start=True, stop=True)
                    moved.then_inc(gathered, 1)

            def mask(image):
                pe.wait_ge(chosen_ready, image + 1)
                for t in range(TILES):
                    moved = nc.tensor.matmul(mask_bank[:, t * COLS:(t + 1) * COLS],
                                             chosen[:, t * TILE_CH:(t + 1) * TILE_CH, :]
                                             .rearrange("p c b -> p (c b)"),
                                             same_band16[0:PATCHES, :], start=True, stop=True)
                moved.then_inc(mask_ready, 1)

            pe.wait_ge(constants, CONSTANTS)
            image_tiles(0)
            with pe.Fori(1, IMAGES) as image:
                image_tiles(image)
            variances(IMAGES - 1)
            gather(IMAGES - 1)
            mask(IMAGES - 1)

        @block.scalar
        def _(act):
            def sums_of(tile, buffer, r, order):
                centred_seen = 0
                last_diff = [x for x in order if x[0] == "diff"][-1]
                rows = buffer[:].rearrange("p (r w) -> p r w", w=WIDTH)
                act.wait_ge(recorded, tile - 1 + CREDIT_RECORDED)
                for kind, n in order:
                    if kind == "diff":
                        item, side = divmod(n, 2)
                        slot, which, w = DIFF_ITEMS[item]
                        if side == 0:
                            act.wait_ge(diff_ready, ITEMS * tile + item + 1)
                        v = diff[slot][:, :, side * PATCH:(side + 1) * PATCH]
                        w += side
                        done = nc.scalar.activation(v, v, ACT.Abs, accum_out=sums[r][:, which, w:w + 1])
                        if side == 1:
                            done.then_inc(diff_free, ITEMS - item if (kind, n) == last_diff else 1)
                    elif kind == "vertical":
                        act.wait_ge(vertical_ready, PE_PATCHES * tile + n + 1)
                        v = vertical[n % 2][:]
                        done = nc.scalar.activation(v, v, ACT.Abs, accum_out=sums[r][:, 1, n:n + 1])
                        done.then_inc(vertical_free, 1)
                    else:
                        k = centred_seen
                        centred_seen += 1
                        if k == 0:
                            act.wait_ge(minus_mean_ready, tile + 1)
                        if k == 0:
                            act.wait_ge(analysed, tile)
                        else:
                            act.wait_ge(centred, (COLS - 1) * tile + k)
                        if (kind, n) == order[-1] and last_diff != ACT_LAST_DIFF:
                            act.wait_ge(diff_ready, ITEMS * tile + ITEMS)
                        done = nc.scalar.activation(junk[:], rows[:, :, n * PATCH:(n + 1) * PATCH], ACT.Abs,
                                                    bias=record[r][:, 2:3], accum_out=sums[r][:, 2, n:n + 1])
                        done.then_inc(analysed if (kind, n) == order[-1] else centred, 1)

            act.wait_ge(constants, CONSTANTS)
            with act.Fori(0, LOOPED) as g:
                for u in range(RING):
                    sums_of(RING * g + u, ring[u], u, ACT_ORDER_FIRST)
            sums_of(LAST, kept, RING, ACT_ORDER_FIRST)
            with act.Fori(1, IMAGES) as image:
                with act.Fori(0, LOOPED) as g:
                    for u in range(RING):
                        sums_of(TILES * image + RING * g + u, ring[u], u, ACT_ORDER)
                sums_of(TILES * image + LAST, kept, RING, ACT_ORDER)

        @block.vector
        def _(dve):
            def settle():
                dve.drain()

            def statistics(tile, buffer, r, loaded, count):
                if loaded is not first_loaded:
                    dve.wait_ge(loaded, 16 * count)
                for k in range(CHUNKS):
                    if loaded is first_loaded and k * len(loaded) % CHUNKS == 0:
                        dve.wait_ge(loaded[k * len(loaded) // CHUNKS], 16)
                    nc.vector.bn_stats(stats[:, k, :], buffer[:, k * BN:(k + 1) * BN])
                settle()
                nc.vector.bn_aggr(record[r][:, 0:2], stats[:]).then_inc(stats_ready, 1)

            def minus_mean(tile, r):
                dve.wait_ge(mean_ready, tile + 1)
                nc.vector.tensor_scalar(record[r][:, 2:3], mean_bank[:, 0:1], -1.0, None, ALU.mult)\
                    .then_inc(minus_mean_ready, 1)

            def differences(tile, buffer, r, items):
                rows = buffer[:].rearrange("p (r w) -> p r w", w=WIDTH)
                nm = record[r][:, 2:3]
                wide = 2 * PATCH
                for item in items:
                    slot, which, w = DIFF_ITEMS[item]
                    d = diff[slot]
                    left_col = w * PATCH
                    dve.wait_ge(diff_free, ITEMS * tile + DIFF_BEFORE[item] + CREDIT_DIFF)
                    if which == 0:
                        lo = 1 if w == 0 else 0
                        hi = wide - 1 if w == COLS - 2 else wide
                        if w == 0:
                            nc.vector.tensor_scalar(d[:, :, 0:1], rows[:, :, 1:2], nm, None, ALU.add)
                        if w == COLS - 2:
                            nc.vector.tensor_scalar(d[:, :, hi:], rows[:, :, WIDTH - 2:WIDTH - 1], nm, None, ALU.add)
                        nc.vector.tensor_tensor(d[:, :, lo:hi], rows[:, :, left_col + lo + 1:left_col + hi + 1],
                                                rows[:, :, left_col + lo - 1:left_col + hi - 1], ALU.subtract)\
                            .then_inc(diff_ready, 1)
                    else:
                        c = slice(left_col, left_col + wide)
                        dve.wait_ge(halo_ready, tile + 1)
                        nc.vector.tensor_tensor(d[:, 0, :], rows[:, 1, c], halo_bank[:, 0, 0:wide], ALU.add)
                        nc.vector.tensor_tensor(d[:, PATCH - 1, :], rows[:, PATCH - 2, c], halo_bank[:, 1, 0:wide],
                                                ALU.add).then_inc(halo_free, 1)
                        nc.vector.tensor_tensor(d[:, 1:PATCH - 1, :], rows[:, 2:PATCH, c], rows[:, 0:PATCH - 2, c],
                                                ALU.subtract).then_inc(diff_ready, 1)

            def read_sums(tile, r):
                dve.wait_ge(analysed, tile + 1)
                nc.vector.tensor_reduce(record[r][:, 3:REC], sums[r][:].rearrange("p k w -> p w k"), AX.X, ALU.add)

            def keep_record(r, t):
                nc.vector.tensor_scalar(records[:, bass.ds(t, 1), :].rearrange("p a k -> p (a k)"), record[r][:],
                                        1.0, None, ALU.mult).then_inc(recorded, 1)

            def fetch_coefficients(t):
                nc.vector.tensor_scalar(coef_now[:].rearrange("p a w -> p (a w)"),
                                        coef[:, bass.ds(t, 1)].rearrange("p t a w -> p (t a w)"),
                                        1.0, None, ALU.mult)

            def apply(pixels, signal):
                rows = pixels.rearrange("p (r w) -> p r w", w=WIDTH)
                for w in range(COLS):
                    v = rows[:, :, w * PATCH:(w + 1) * PATCH]
                    done = nc.vector.tensor_scalar(v, v, coef_now[:, 0, w:w + 1], coef_now[:, 1, w:w + 1],
                                                   ALU.mult, ALU.add)
                done.then_inc(signal, 1)

            def apply_again(image, g, w):
                dve.wait_ge(again_loaded[w % SLOTS],
                            16 * (2 * LOOPED * image - 2 * LOOPED + 2 * g + w // SLOTS + 1))
                apply(again[w % SLOTS][:], applied)

            def sum_last_item(r):
                slot, which, w = DIFF_ITEMS[-1]
                nc.vector.tensor_reduce(sums[r][:, which, w:w + 2],
                                        diff[slot][:].rearrange("p r (w c) -> p w r c", w=2), AX.XY, ALU.add,
                                        apply_absolute_value=True)

            def step(image, g, u, before, after, count, output):
                tile = TILES * image + RING * g + u
                place = RING if after is None else u
                early = EARLY_ITEMS if isinstance(g, int) and g == 0 and u == 0 else 0
                if not early:
                    settle()
                differences(tile, places[place], place, range(early, ITEMS))
                if before is not None:
                    read_sums(tile - 1, before)
                if output:
                    fetch_coefficients(RING * g + u - 1)
                settle()
                if before is not None:
                    keep_record(before, RING * g + u - 1)
                if output:
                    apply_again(image, g, 2 * u - 2)
                elif isinstance(image, int):
                    sum_last_item(place)
                if after is None:
                    nc.vector.tensor_scalar(records[:, LAST, 0:3], record[RING][:, 0:3], 1.0, None, ALU.mult)
                else:
                    statistics(tile + 1, places[after], after, place_loaded[after], count)
                if output:
                    apply_again(image, g, 2 * u - 1)
                if after is not None:
                    minus_mean(tile + 1, after)

            def image_tiles(image, output):
                loads = [LOOPED * image - (b == 0) for b in range(RING)]
                step(image, 0, 0, None, 1, loads[1] + 1, False)
                step(image, 0, 1, 0, 2, loads[2] + 1, output)
                step(image, 0, 2, 1, 0, loads[0] + 2, output)
                with dve.Fori(1, LOOPED - 1) as g:
                    for u in range(RING):
                        b = (u + 1) % RING
                        step(image, g, u, (u - 1) % RING, b, loads[b] + g + (u + 1) // RING + 1, output)
                step(image, LOOPED - 1, 0, RING - 1, 1, loads[1] + LOOPED, output)
                step(image, LOOPED - 1, 1, 0, 2, loads[2] + LOOPED, output)
                step(image, LOOPED - 1, 2, 1, RING, image + 1, output)
                step(image, LOOPED - 1, RING, RING - 1, None, None, output)

            part_mean, part_var, nm = (records[:, :, k] for k in range(3))

            def partition_spread():
                settle()
                nc.vector.tensor_tensor(spread2[:], part_mean, nm, ALU.add)
                settle()
                nc.vector.tensor_tensor(newton[:], spread2[:], spread2[:], ALU.mult)
                settle()
                nc.vector.tensor_tensor(spread[:], newton[:], part_var, ALU.add).then_inc(spread_ready, 1)

            def stable_variance(image):
                dve.wait_ge(var_ready, image + 1)
                nc.vector.tensor_scalar(var[:], var_bank, EPS, None, ALU.add).then_inc(stable_var_ready, 1)

            def score(sums_part, tiles, n):
                scale3 = scale[:, tiles].unsqueeze(2).broadcast_to([PARTS, n, COLS])
                nc.vector.tensor_tensor(scores[:, tiles], sums_part, scale3, ALU.mult)
                settle()
                nc.vector.tensor_tensor(by_band[:, tiles],
                                        scores[:, tiles].unsqueeze(2).broadcast_to([PARTS, n, BANDS, COLS]),
                                        same_band[:].unsqueeze(1).unsqueeze(3)
                                        .broadcast_to([PARTS, n, BANDS, COLS]),
                                        ALU.mult).then_inc(by_band_ready, 1)

            def score_most(image):
                dve.wait_ge(rstd_ready, image + 1)
                nc.vector.tensor_tensor(newton[:], rstd[:], rstd[:], ALU.mult)
                settle()
                nc.vector.tensor_tensor(spread2[:], newton[:], var[:], ALU.mult)
                settle()
                nc.vector.tensor_scalar(newton[:], spread2[:], -0.5, 1.5, ALU.mult, ALU.add)
                settle()
                nc.vector.tensor_tensor(scale[:], rstd[:], newton[:], ALU.mult)
                settle()
                dve.wait_ge(diff_free, ITEMS * (TILES * image + LAST) + VERTICAL_ITEM + 1 + CREDIT_DIFF)
                score(records[:, 0:LAST, 3:REC], slice(0, LAST), LAST)

            def rank(image):
                read_sums(TILES * image + LAST, RING)
                settle()
                nc.vector.tensor_scalar(records[:, LAST, 3:REC], record[RING][:, 3:REC], 1.0, None, ALU.mult)\
                    .then_inc(recorded, 1)
                settle()
                score(records[:, LAST:TILES, 3:REC], slice(LAST, TILES), 1)
                scale3 = scale[:].unsqueeze(2).broadcast_to([PARTS, TILES, COLS])
                dve.wait_ge(gathered, 2 * image + 2)
                nc.vector.tensor_copy(left, score_bank[0:PATCHES, :])
                settle()
                with dve.Fori(0, ROUNDS // ROUNDS_UNROLLED):
                    for _ in range(ROUNDS_UNROLLED):
                        nc.vector.max(largest[:], left)
                        settle()
                        nc.vector.match_replace(out=left, in_to_replace=largest[:], in_values=left,
                                                imm_value=-1.0)
                        settle()
                nc.vector.scalar_tensor_tensor(out=chosen,
                                               in0=left.unsqueeze(2).broadcast_to([PATCHES, CHANNELS, BANDS]),
                                               scalar=0.0,
                                               in1=same_channel[0:PATCHES, 0:BANDS].unsqueeze(1)
                                               .broadcast_to([PATCHES, CHANNELS, BANDS]),
                                               op0=ALU.is_lt, op1=ALU.mult).then_inc(chosen_ready, 1)
                dve.wait_ge(mask_ready, image + 1)
                nc.vector.tensor_tensor(scores[:],
                                        mask_bank.rearrange("p (t w) -> p t w", w=COLS),
                                        scale3, ALU.mult)
                settle()
                nc.vector.tensor_scalar(coef[:, :, 0, :], scores[:], 1.0, None, ALU.add)
                nc.vector.tensor_tensor(coef[:, :, 1, :], scores[:],
                                        nm.unsqueeze(2).broadcast_to([PARTS, TILES, COLS]), ALU.mult)
                settle()

            places = [*ring, kept]
            place_loaded = [*ring_loaded, kept_loaded]

            dve.wait_ge(constants, CONSTANTS)
            nc.vector.tensor_reduce(same_band[:], plus[:].rearrange("p (c b) -> p b c", b=BANDS), AX.X, ALU.add)
            settle()
            nc.vector.tensor_copy(same_band16[:], same_band[:])

            statistics(0, ring[0], 0, first_loaded, 1)
            minus_mean(0, 0)
            settle()
            differences(0, ring[0], 0, range(EARLY_ITEMS))
            image_tiles(0, False)
            with dve.Fori(1, IMAGES) as image:
                partition_spread()
                statistics(TILES * image, ring[0], 0, ring_loaded[0], LOOPED * image)
                stable_variance(image - 1)
                minus_mean(TILES * image, 0)
                settle()
                differences(TILES * image, ring[0], 0, range(EARLY_ITEMS))
                score_most(image - 1)
                rank(image - 1)
                fetch_coefficients(LAST)
                settle()
                apply(kept[:, 0:HALF], applied)
                apply(kept[:, HALF:PIX], applied)
                image_tiles(image, True)
            partition_spread()
            stable_variance(IMAGES - 1)
            score_most(IMAGES - 1)
            rank(IMAGES - 1)

            for n, t in enumerate(order):
                settle()
                fetch_coefficients(t)
                settle()
                apply(buffers[n][:], finished)
            settle()
            fetch_coefficients(0)
            settle()
            for h in range(2):
                dve.wait_ge(again_loaded[h], 16 * (2 * LOOPED * (IMAGES - 1) + 1))
                apply(again[h][:], finished)

            def finish(tile, b, loads):
                settle()
                fetch_coefficients(tile)
                settle()
                dve.wait_ge(refilled[b], 16 * loads)
                apply(buffers[b][:], finished)

            with dve.Fori(0, REFILLS // BUFFERS) as k:
                for b in range(BUFFERS):
                    finish(BUFFERS * k + b + 1, b, k + 1)
            for n in range(REFILLS // BUFFERS * BUFFERS, REFILLS):
                finish(n + 1, n % BUFFERS, n // BUFFERS + 1)


def kernel(**inputs):
    import numpy as _np
    import concourse.bacc as _bacc
    from concourse import mybir as _mybir
    from concourse.bass_utils import run_bass_kernel_spmd as _run

    nc = _bacc.Bacc("TRN2", target_bir_lowering=False, num_devices=1)
    a = _np.ascontiguousarray(inputs["x"])
    shape = a.shape
    a = a.reshape(IMAGES * TILES, PARTS, PIX)
    x = nc.dram_tensor("in_x_dram", a.shape, _mybir.dt.from_np(a.dtype), kind="ExternalInput").ap()
    out = nc.dram_tensor("out_0_dram", a.shape, _mybir.dt.from_np(a.dtype), kind="ExternalOutput").ap()
    groupnorm_patch_topk(nc, x, out)
    r = _run(nc, [{"in_x_dram": a}], core_ids=[0])
    return r.results[0]["out_0_dram"].reshape(shape)
```

```python
import concourse.bass as bass
from concourse import mybir
from contextlib import ExitStack

FP32 = mybir.dt.float32
BF16 = mybir.dt.bfloat16
ALU = mybir.AluOpType
ACT = mybir.ActivationFunctionType
AX = mybir.AxisListType

IMAGES, CHANNELS, HEIGHT, WIDTH = 4, 256, 256, 256
GROUPS = 32
PATCH = 32
KEPT = CHANNELS // 2
EPS = 1e-5

PARTS = 128
BANDS = HEIGHT // PATCH
COLS = WIDTH // PATCH
TILE_CH = PARTS // BANDS
TILES = CHANNELS // TILE_CH
PIX = PATCH * WIDTH
HALF = PIX // 2
GROUP_PARTS = CHANNELS // GROUPS * BANDS
PATCHES = BANDS * COLS

RING = 3
SLOTS = 3
LOOPED = (TILES - 1) // RING
LAST = TILES - 1
BN = 512
CHUNKS = PIX // BN

PE_PATCHES = 5
ITEMS = 6
ROUNDS = KEPT // 8
ROUNDS_UNROLLED = 4
DIFF_ITEMS = [(0, 0, [0, 1]), (1, 0, [2, 3]), (2, 1, [6, 7]), (0, 0, [4, 5]), (1, 0, [6, 7]), (2, 1, [PE_PATCHES])]
EARLY_ITEMS = 2
HALVES = 2 * (TILES - 1)
OUTPUT = ([(1, 0, 1), (0, 1, 0), (0, 1, 0)], (0, 1, 1), [(0, 1, 1), (0, 1, 0), (0, 1, 0), (0, 1, 2)], 1)
OUTPUT_OF_LAST = ([(1, 0, 1), (0, 1, 0), (0, 1, 0)], (0, 1, 1), [(0, 1, 1), (0, 1, 1), (0, 1, 1), (0, 1, 0)], 1)
LOADED_AT_ONCE = SLOTS
DIFF_BEFORE = [-2, -1, 0, 1, 2, 3]
ACT_ORDER = [("diff", 0, 0), ("diff", 0, 1), ("diff", 1, 2), ("diff", 1, 3), ("vertical", 0),
             ("diff", 2, 6), ("diff", 2, 7), ("centred", 0), ("vertical", 1),
             ("diff", 3, 4), ("diff", 3, 5), ("centred", 1), ("vertical", 2), ("centred", 2), ("centred", 3),
             ("diff", 4, 6), ("diff", 4, 7), ("vertical", 3), ("diff", 5, PE_PATCHES), ("centred", 4),
             ("vertical", 4), ("centred", 5), ("centred", 6), ("centred", 7)]
ACT_ORDER_LAST = [("diff", 0, 0), ("diff", 0, 1), ("diff", 1, 2), ("diff", 1, 3), ("vertical", 0),
                  ("diff", 2, 6), ("diff", 2, 7), ("centred", 0), ("vertical", 1), ("centred", 1), ("centred", 2),
                  ("centred", 3), ("vertical", 2), ("centred", 4), ("centred", 5), ("vertical", 3), ("centred", 6),
                  ("vertical", 4), ("centred", 7)]
OWN_SUMS_FIRST, OWN_SUMS_LAST, OWN_SUMS = 1, 3, 0


def output_plan(counts):
    first, looped, last, ranking = counts

    def number(steps, start):
        halves = []
        for step in steps:
            halves.append([])
            for n in step:
                halves[-1].append(list(range(start, start + n)))
                start += n
        return halves, start

    first, start = number(first, 0)
    looped, end = number([looped] * RING, start - 2 * RING)
    assert end == start
    last, end = number(last, end - 2 * RING)
    ranking = list(range(end, end + ranking))
    assert 2 * RING * (LOOPED - 1) + end + len(ranking) == HALVES
    return first, looped, last, ranking


REC = 3 + COLS


def groupnorm_patch_topk(nc: bass.Bass, x: bass.AP, out: bass.AP):
    ctx = ExitStack()
    with ctx:
        def sb(name, shape, dt=FP32):
            return ctx.enter_context(nc.sbuf_tensor(name, shape, dt))

        def pb(name, shape, dt=FP32):
            return ctx.enter_context(nc.psum_tensor(name, shape, dt))

        def sem(name):
            return ctx.enter_context(nc.semaphore(name))

        ring = [sb(f"ring{b}", [PARTS, PIX]) for b in range(RING)]
        kept = sb("kept", [PARTS, PIX])
        again = [sb(f"again{b}", [PARTS, HALF]) for b in range(SLOTS)]
        diff = [sb(f"diff{b}", [PARTS, PATCH, 2 * PATCH]) for b in range(3)]

        plus = sb("plus", [PARTS, PARTS])
        minus = sb("minus", [PARTS, PARTS])
        from_above = sb("from_above", [PARTS, PARTS])
        from_below = sb("from_below", [PARTS, PARTS])
        at_top = sb("at_top", [PARTS, PARTS])
        at_bottom = sb("at_bottom", [PARTS, PARTS])
        averager = sb("averager", [PARTS, PARTS])
        same_channel = sb("same_channel", [PARTS, TILE_CH])
        same_band = sb("same_band", [PARTS, BANDS])
        same_band16 = sb("same_band16", [PARTS, BANDS], BF16)
        scale = sb("scale", [PARTS, TILES])
        minus_half = sb("minus_half", [PARTS, TILES])

        stats = sb("stats", [PARTS, CHUNKS, 6])
        record = [sb(f"record{b}", [PARTS, 3]) for b in range(RING + 1)]
        sums = [sb(f"sums{b}", [PARTS, 3, COLS]) for b in range(RING + 1)]
        records = sb("records", [PARTS, TILES, REC])
        spread = sb("spread", [PARTS, TILES])
        spread2 = sb("spread2", [PARTS, TILES])
        var = sb("var", [PARTS, TILES])
        rstd = sb("rstd", [PARTS, TILES])
        newton = sb("newton", [PARTS, TILES])
        scores = sb("scores", [PARTS, TILES, COLS])
        largest = sb("largest", [PATCHES, 8])
        coef = sb("coef", [PARTS, TILES, 2, COLS])
        coef_now = sb("coef_now", [PARTS, 2, COLS])

        vertical = [pb(f"vertical{b}", [PARTS, PATCH, PATCH]) for b in range(2)]
        small_bank = pb("small_bank", [PARTS, 512])
        halo_bank = small_bank[:, 0:2 * (COLS - PE_PATCHES) * PATCH].rearrange("p (a w) -> p a w", a=2)
        mean_bank = small_bank[:, 256:512]
        rank_bank = pb("rank_bank", [PARTS, 512])
        score_bank = rank_bank[:, 0:CHANNELS]
        mask_bank = rank_bank[:, CHANNELS:CHANNELS + TILES * COLS]
        var_bank = rank_bank[:, CHANNELS + TILES * COLS:CHANNELS + TILES * COLS + TILES]
        junk = pb("junk", [PARTS, PATCH, PATCH])
        idle = diff[2][:].rearrange("p r w -> p (r w)")
        spread_cols = TILES * PATCHES
        by_band = idle[:, 0:spread_cols].rearrange("p (t b w) -> p t b w", b=BANDS, w=COLS)
        chosen = idle[0:PATCHES, spread_cols:].bitcast(BF16).rearrange("p (c b) -> p c b", b=BANDS)
        left = coef[0:PATCHES].rearrange("p t a w -> p (t a w)")

        constants = sem("constants")
        first_loaded = [sem(f"first_loaded{k}") for k in range(4)]
        ring_loaded = [sem(f"ring_loaded{b}") for b in range(RING)]
        kept_loaded = sem("kept_loaded")
        again_loaded = [sem(f"again_loaded{b}") for b in range(SLOTS)]
        again_stored = [sem(f"again_stored{b}") for b in range(SLOTS)]
        kept_stored = sem("kept_stored")
        stats_ready = sem("stats_ready")
        mean_ready = sem("mean_ready")
        minus_mean_ready = sem("minus_mean_ready")
        halo_ready = sem("halo_ready")
        halo_free = sem("halo_free")
        diff_ready = sem("diff_ready")
        diff_free = sem("diff_free")
        vertical_ready = sem("vertical_ready")
        vertical_free = sem("vertical_free")
        analysed = sem("analysed")
        centred = sem("centred")
        recorded = sem("recorded")
        spread_ready = sem("spread_ready")
        var_ready = sem("var_ready")
        stable_var_ready = sem("stable_var_ready")
        rstd_ready = sem("rstd_ready")
        by_band_ready = sem("by_band_ready")
        gathered = sem("gathered")
        chosen_ready = sem("chosen_ready")
        mask_ready = sem("mask_ready")
        applied = sem("applied")

        finished = sem("finished")
        buffers = [kept, *ring]
        BUFFERS = len(buffers)
        REFILLS = TILES - BUFFERS - 2
        order = [LAST, *range(LAST - RING, LAST)]
        finished_stored = [sem(f"finished_stored{b}") for b in range(len(buffers))]
        refilled = [sem(f"refilled{b}") for b in range(len(buffers))]

        block = ctx.enter_context(nc.Block())

        CONSTANTS = 21
        PER_IMAGE = 2 * TILES
        CREDIT_DIFF, CREDIT_VERTICAL, CREDIT_HALO, CREDIT_RECORDED = ITEMS, 2, 1, 2
        CREDIT_STORED = 16

        @block.gpsimd
        def _(pool):
            steps = [0]

            def make(ins):
                steps[0] += 1
                ins.then_inc(constants, 1)
                pool.wait_ge(constants, steps[0])

            def diagonal(columns, count, step, base, value):
                make(nc.gpsimd.affine_select(out=columns, in_=columns, compare_op=ALU.not_equal, fill=value,
                                             base=base, pattern=[[-step, count]], channel_multiplier=1))

            def bands(m, band):
                return m[:].rearrange("p (c b) -> p c b", b=BANDS)[:, :, band]

            pool.sem_inc(diff_free, CREDIT_DIFF)
            pool.sem_inc(vertical_free, CREDIT_VERTICAL)
            pool.sem_inc(halo_free, CREDIT_HALO)
            pool.sem_inc(recorded, CREDIT_RECORDED)
            for stored in (*again_stored, kept_stored):
                pool.sem_inc(stored, CREDIT_STORED)
            make(nc.gpsimd.memset(minus_half[:], -0.5))
            make(nc.gpsimd.memset(same_channel[:], 1.0))
            make(nc.gpsimd.memset(averager[:], 0.0))
            make(nc.gpsimd.memset(plus[:], 0.0))
            for m in (minus, from_above, from_below, at_top, at_bottom):
                make(nc.gpsimd.memset(m[:], 0.0))
            for first in range(0, PARTS, GROUP_PARTS):
                make(nc.gpsimd.memset(averager[first:first + GROUP_PARTS, first:first + GROUP_PARTS],
                                      1.0 / GROUP_PARTS))
            diagonal(plus[:], PARTS, 1, 0, 1.0)
            diagonal(minus[:], PARTS, 1, 0, -1.0)
            diagonal(bands(at_top, 0), TILE_CH, BANDS, 0, 1.0)
            diagonal(bands(at_bottom, BANDS - 1), TILE_CH, BANDS, 1 - BANDS, 1.0)
            diagonal(from_above[:], PARTS, 1, 1, -1.0)
            diagonal(from_below[:], PARTS, 1, -1, -1.0)
            make(nc.gpsimd.memset(bands(from_above, 0), 0.0))
            make(nc.gpsimd.memset(bands(from_below, BANDS - 1), 0.0))
            make(nc.gpsimd.affine_select(out=same_channel[:], in_=same_channel[:], compare_op=ALU.is_ge, fill=0.0,
                                         base=0, pattern=[[-BANDS, TILE_CH]], channel_multiplier=1))
            make(nc.gpsimd.affine_select(out=same_channel[:], in_=same_channel[:], compare_op=ALU.is_ge, fill=0.0,
                                         base=BANDS - 1, pattern=[[BANDS, TILE_CH]], channel_multiplier=-1))
            assert steps[0] == CONSTANTS

            with pool.Fori(0, IMAGES) as image:
                pool.wait_ge(stable_var_ready, image + 1)
                nc.gpsimd.tensor_tensor(rstd[:], var[:], minus_half[:], ALU.pow).then_inc(rstd_ready, 1)

        @block.sync
        def _(sp):
            def load_tile(tile, buffer, signal):
                sp.dma_start(buffer[:], x[bass.ds(tile, 1)].rearrange("a p f -> p (a f)")).then_inc(signal, 16)

            def load_half(tile, half, slot):
                sp.dma_start(again[slot][:], x[bass.ds(tile, 1), :, half * HALF:(half + 1) * HALF]
                             .rearrange("a p f -> p (a f)")).then_inc(again_loaded[slot], 16)

            def store_tile(tile, buffer, signal):
                sp.dma_start(out[bass.ds(tile, 1)].rearrange("a p f -> p (a f)"), buffer[:]).then_inc(signal, 16)

            def store_half(tile, half, source, signal):
                sp.dma_start(out[bass.ds(tile, 1), :, half * HALF:(half + 1) * HALF]
                             .rearrange("a p f -> p (a f)"), source).then_inc(signal, 16)

            def load_two_ahead(image, g, u, last=False):
                tile = TILES * image + RING * g + u
                if isinstance(g, int) and RING * g + u == LAST - 2:
                    sp.wait_ge(kept_stored, 32 * image + CREDIT_STORED)
                    load_tile(tile + 2, kept, kept_loaded)
                elif isinstance(g, int) and RING * g + u > LAST - 2:
                    b = RING * g + u - LAST + 1
                    if not last:
                        sp.wait_ge(analysed, tile - 1)
                        load_tile(tile + 2, ring[b], ring_loaded[b])
                else:
                    sp.wait_ge(analysed, tile)
                    load_tile(tile + 2, ring[(u + 2) % RING], ring_loaded[(u + 2) % RING])

            def load_again(image, g, w, ahead=0):
                sp.wait_ge(again_stored[w % SLOTS],
                           16 * (2 * LOOPED * image + 2 * g + (2 * LOOPED * (ahead - 1) + w // SLOTS))
                           + CREDIT_STORED)
                load_half(TILES * image + RING * g + (TILES * (ahead - 1) + w // 2), w % 2, w % SLOTS)

            def load_first_again(image, halves):
                for w in range(halves):
                    load_again(image, 0, w, 1)

            def finish_halves(image, g, halves):
                for w in halves:
                    sp.wait_ge(applied, PER_IMAGE * image + 2 * RING * g + (w + 3 - PER_IMAGE))
                    store_half(TILES * (image - 1) + (RING * g + w // 2), w % 2, again[w % SLOTS][:],
                               again_stored[w % SLOTS])
                    peeled = isinstance(g, int)
                    if not (peeled and (2 * RING * g + w + 2 >= HALVES or 2 * RING * g + w + 2 < LOADED_AT_ONCE)):
                        load_again(image, g, w + 2)

            def image_loads(image, last):
                load_two_ahead(image, 0, 0)
                for h in range(2):
                    sp.wait_ge(applied, PER_IMAGE * image - PER_IMAGE + h + 1)
                    store_half(TILES * image - 1, h, kept[:, h * HALF:(h + 1) * HALF], kept_stored)
                first_steps, looped_steps, last_steps, ranking = output_plan(OUTPUT_OF_LAST if last else OUTPUT)
                for u in range(RING):
                    if u:
                        load_two_ahead(image, 0, u)
                    finish_halves(image, 0, sum(first_steps[u], []))
                with sp.Fori(1, LOOPED - 1) as g:
                    for u in range(RING):
                        load_two_ahead(image, g, u)
                        finish_halves(image, g, sum(looped_steps[u], []))
                for u in range(RING + 1):
                    load_two_ahead(image, LOOPED - 1, u, last)
                    finish_halves(image, LOOPED - 1, sum(last_steps[u], []))
                finish_halves(image, LOOPED - 1, ranking)
                load_first_again(image, LOADED_AT_ONCE)

            for quarter, loaded in enumerate(first_loaded):
                part = slice(quarter * PIX // 4, (quarter + 1) * PIX // 4)
                sp.dma_start(ring[0][:, part], x[0, :, part]).then_inc(loaded, 16)
            load_tile(1, ring[1], ring_loaded[1])
            load_tile(2, ring[2], ring_loaded[2])
            load_two_ahead(0, 0, 1)
            load_two_ahead(0, 0, 2)
            load_first_again(0, LOADED_AT_ONCE)
            with sp.Fori(1, LOOPED - 1) as g:
                for u in range(RING):
                    load_two_ahead(0, g, u)
            for u in range(RING + 1):
                load_two_ahead(0, LOOPED - 1, u)
            with sp.Fori(1, IMAGES - 1) as image:
                image_loads(image, False)
            image_loads(IMAGES - 1, True)

            base = TILES * (IMAGES - 1)

            def refill(n):
                b = n % BUFFERS
                if n == 0:
                    sp.wait_ge(kept_stored, 32 * (IMAGES - 1) + 16 + CREDIT_STORED)
                sp.wait_ge(finished_stored[b], 16 * (n // BUFFERS + 1))
                load_tile(base + n + 2, buffers[b], refilled[b])

            def finish_again(q, count):
                sp.wait_ge(finished, count)
                store_half(base + q // 2, q % 2, again[q % SLOTS][:], again_stored[q % SLOTS])

            sp.wait_ge(applied, PER_IMAGE * (IMAGES - 1) + 1)
            store_half(base + LAST, 0, kept[:, 0:HALF], kept_stored)
            sp.wait_ge(finished, 1)
            store_half(base + LAST, 1, kept[:, HALF:PIX], finished_stored[0])
            for n in range(1, BUFFERS):
                sp.wait_ge(finished, n + 1)
                store_tile(base + order[n], buffers[n], finished_stored[n])
                refill(n - 1)
            for q in range(SLOTS):
                finish_again(q, BUFFERS + q + 1)
            load_again(IMAGES - 1, 0, SLOTS, 1)
            counted = BUFFERS + SLOTS
            for n in range(REFILLS):
                sp.wait_ge(finished, counted + n + 1)
                store_tile(base + n + 2, buffers[n % BUFFERS], finished_stored[n % BUFFERS])
                if n + BUFFERS - 1 < REFILLS:
                    refill(n + BUFFERS - 1)
            finish_again(SLOTS, counted + REFILLS + 1)
            for b in range(BUFFERS):
                sp.wait_ge(finished_stored[b], 16 * (1 + len(range(b, REFILLS, BUFFERS))))
            for slot in range(SLOTS):
                sp.wait_ge(again_stored[slot],
                           16 * (2 * LOOPED * (IMAGES - 1) + (2 if slot == 0 else 1)) + CREDIT_STORED)
            sp.wait_ge(kept_stored, 32 * (IMAGES - 1) + 16 + CREDIT_STORED)

        @block.tensor
        def _(pe):
            def mean(tile, r):
                pe.wait_ge(stats_ready, tile + 1)
                nc.tensor.matmul(mean_bank[:, 0:1], averager[:], record[r][:, 0:1], start=True, stop=True)\
                    .then_inc(mean_ready, 1)

            def border(target, matrix, halo, edge, minus_mean, accumulate):
                n = halo.shape[1]
                nc.tensor.matmul(target, matrix[:], halo, start=not accumulate, stop=False)
                return nc.tensor.matmul(target, edge[:], minus_mean.broadcast_to([PARTS, n]), start=False, stop=True)

            def halo(tile, buffer, r):
                rows = buffer[:].rearrange("p (r w) -> p r w", w=WIDTH)
                pe.wait_ge(minus_mean_ready, tile + 1)
                pe.wait_ge(halo_free, tile + CREDIT_HALO)
                first = PE_PATCHES * PATCH
                border(halo_bank[:, 0, 0:WIDTH - first], from_above, rows[:, PATCH - 1, first:], at_top,
                       record[r][:, 2:3], False)
                border(halo_bank[:, 1, 0:WIDTH - first], from_below, rows[:, 0, first:], at_bottom,
                       record[r][:, 2:3], False).then_inc(halo_ready, 1)

            def differences(tile, buffer, r, patches):
                rows = buffer[:].rearrange("p (r w) -> p r w", w=WIDTH)
                minus_mean = record[r][:, 2:3]
                mid = PATCH // 2
                for w in patches:
                    c = slice(w * PATCH, (w + 1) * PATCH)
                    v = vertical[w % 2]
                    pe.wait_ge(vertical_free, PE_PATCHES * tile + max(w - 1, 0) + CREDIT_VERTICAL)
                    nc.tensor.matmul(v[:, 0:mid, :], plus[:], rows[:, 1:mid + 1, c], start=True, stop=False)
                    nc.tensor.matmul(v[:, 1:mid, :], minus[:], rows[:, 0:mid - 1, c], start=False, stop=False)
                    border(v[:, 0, :], from_above, rows[:, PATCH - 1, c], at_top, minus_mean, True)
                    nc.tensor.matmul(v[:, mid:PATCH, :], plus[:], rows[:, mid - 1:PATCH - 1, c],
                                     start=True, stop=False)
                    nc.tensor.matmul(v[:, mid:PATCH - 1, :], minus[:], rows[:, mid + 1:PATCH, c],
                                     start=False, stop=False)
                    border(v[:, PATCH - 1, :], from_below, rows[:, 0, c], at_bottom, minus_mean, True)\
                        .then_inc(vertical_ready, 1)

            def tile_work(tile, buffer, r, after):
                halo(tile, buffer, r)
                differences(tile, buffer, r, range(PE_PATCHES))
                mean(tile + 1, after)

            def first_tile(image):
                tile = TILES * image
                ranking = not isinstance(image, int)
                mean(tile, 0)
                halo(tile, ring[0], 0)
                if ranking:
                    gather(image - 1)
                differences(tile, ring[0], 0, range(0, 3))
                if ranking:
                    mask(image - 1)
                differences(tile, ring[0], 0, range(3, PE_PATCHES))
                mean(tile + 1, 1)

            def image_tiles(image):
                first_tile(image)
                tile_work(TILES * image + 1, ring[1], 1, 2)
                tile_work(TILES * image + 2, ring[2], 2, 0)
                with pe.Fori(1, LOOPED - 1) as g:
                    for u in range(RING):
                        tile_work(TILES * image + RING * g + u, ring[u], u, (u + 1) % RING)
                for u in range(RING):
                    tile_work(TILES * image + LAST - RING + u, ring[u], u, u + 1)
                halo(TILES * image + LAST, kept, RING)
                differences(TILES * image + LAST, kept, RING, range(PE_PATCHES - 1))
                variances(image)
                differences(TILES * image + LAST, kept, RING, range(PE_PATCHES - 1, PE_PATCHES))

            def variances(image):
                pe.wait_ge(spread_ready, image + 1)
                nc.tensor.matmul(var_bank, averager[:], spread[:], start=True, stop=True).then_inc(var_ready, 1)

            def gather(image):
                for count, tiles in ((1, range(LAST)), (2, [LAST])):
                    pe.wait_ge(by_band_ready, 2 * image + count)
                    for t in tiles:
                        moved = nc.tensor.matmul(score_bank[0:PATCHES, t * TILE_CH:(t + 1) * TILE_CH],
                                                 by_band[:, t].rearrange("p b w -> p (b w)"), same_channel[:],
                                                 start=True, stop=True)
                    moved.then_inc(gathered, 1)

            def mask(image):
                pe.wait_ge(chosen_ready, image + 1)
                for t in range(TILES):
                    moved = nc.tensor.matmul(mask_bank[:, t * COLS:(t + 1) * COLS],
                                             chosen[:, t * TILE_CH:(t + 1) * TILE_CH, :]
                                             .rearrange("p c b -> p (c b)"),
                                             same_band16[0:PATCHES, :], start=True, stop=True)
                moved.then_inc(mask_ready, 1)

            pe.wait_ge(constants, CONSTANTS)
            image_tiles(0)
            with pe.Fori(1, IMAGES) as image:
                image_tiles(image)
            gather(IMAGES - 1)
            mask(IMAGES - 1)

        @block.scalar
        def _(act):
            def sums_of(tile, buffer, r, order, own_sums):
                last_item = ITEMS - own_sums - 1
                order = [one for one in order if one[0] != "diff" or one[1] <= last_item]
                centred_seen = 0
                rows = buffer[:].rearrange("p (r w) -> p r w", w=WIDTH)
                act.wait_ge(recorded, tile - 1 + CREDIT_RECORDED)
                for one in order:
                    kind, n = one[:2]
                    if kind == "diff":
                        item, w = one[1:]
                        slot, which, columns = DIFF_ITEMS[item]
                        if w == columns[0]:
                            act.wait_ge(diff_ready, ITEMS * tile + item + 1)
                        first = (w - columns[0]) * PATCH
                        v = diff[slot][:, :, first:first + PATCH]
                        done = nc.scalar.activation(v, v, ACT.Abs, accum_out=sums[r][:, which, w:w + 1])
                        if w == columns[-1]:
                            done.then_inc(diff_free, ITEMS - item if item == last_item else 1)
                    elif kind == "vertical":
                        act.wait_ge(vertical_ready, PE_PATCHES * tile + n + 1)
                        v = vertical[n % 2][:]
                        done = nc.scalar.activation(v, v, ACT.Abs, accum_out=sums[r][:, 1, n:n + 1])
                        done.then_inc(vertical_free, 1)
                    else:
                        k = centred_seen
                        centred_seen += 1
                        if k == 0:
                            act.wait_ge(minus_mean_ready, tile + 1)
                        if k == 0:
                            act.wait_ge(analysed, tile)
                        else:
                            act.wait_ge(centred, (COLS - 1) * tile + k)
                        if one is order[-1] and own_sums:
                            act.wait_ge(diff_ready, ITEMS * tile + ITEMS)
                        done = nc.scalar.activation(junk[:], rows[:, :, n * PATCH:(n + 1) * PATCH], ACT.Abs,
                                                    bias=record[r][:, 2:3], accum_out=sums[r][:, 2, n:n + 1])
                        done.then_inc(analysed if one is order[-1] else centred, 1)

            act.wait_ge(constants, CONSTANTS)
            with act.Fori(0, LOOPED) as g:
                for u in range(RING):
                    sums_of(RING * g + u, ring[u], u, ACT_ORDER, OWN_SUMS_FIRST)
            sums_of(LAST, kept, RING, ACT_ORDER_LAST, OWN_SUMS_LAST)
            with act.Fori(1, IMAGES) as image:
                with act.Fori(0, LOOPED) as g:
                    for u in range(RING):
                        sums_of(TILES * image + RING * g + u, ring[u], u, ACT_ORDER, OWN_SUMS)
                sums_of(TILES * image + LAST, kept, RING, ACT_ORDER_LAST, OWN_SUMS_LAST)

        @block.vector
        def _(dve):
            def settle():
                dve.drain()

            def statistics(tile, buffer, r, loaded, count):
                if loaded is not first_loaded:
                    dve.wait_ge(loaded, 16 * count)
                for k in range(CHUNKS):
                    if loaded is first_loaded and k * len(loaded) % CHUNKS == 0:
                        dve.wait_ge(loaded[k * len(loaded) // CHUNKS], 16)
                    nc.vector.bn_stats(stats[:, k, :], buffer[:, k * BN:(k + 1) * BN])
                settle()
                nc.vector.bn_aggr(record[r][:, 0:2], stats[:]).then_inc(stats_ready, 1)

            def minus_mean(tile, r):
                dve.wait_ge(mean_ready, tile + 1)
                nc.vector.tensor_scalar(record[r][:, 2:3], mean_bank[:, 0:1], -1.0, None, ALU.mult)\
                    .then_inc(minus_mean_ready, 1)

            def differences(tile, buffer, r, items):
                rows = buffer[:].rearrange("p (r w) -> p r w", w=WIDTH)
                nm = record[r][:, 2:3]
                for item in items:
                    slot, which, columns = DIFF_ITEMS[item]
                    d = diff[slot]
                    w = columns[0]
                    wide = len(columns) * PATCH
                    left_col = w * PATCH
                    dve.wait_ge(diff_free, ITEMS * tile + DIFF_BEFORE[item] + CREDIT_DIFF)
                    if which == 0:
                        lo = 1 if w == 0 else 0
                        hi = wide - 1 if columns[-1] == COLS - 1 else wide
                        if w == 0:
                            nc.vector.tensor_scalar(d[:, :, 0:1], rows[:, :, 1:2], nm, None, ALU.add)
                        if columns[-1] == COLS - 1:
                            nc.vector.tensor_scalar(d[:, :, hi:], rows[:, :, WIDTH - 2:WIDTH - 1], nm, None, ALU.add)
                        nc.vector.tensor_tensor(d[:, :, lo:hi], rows[:, :, left_col + lo + 1:left_col + hi + 1],
                                                rows[:, :, left_col + lo - 1:left_col + hi - 1], ALU.subtract)\
                            .then_inc(diff_ready, 1)
                    else:
                        c = slice(left_col, left_col + wide)
                        h = slice(left_col - PE_PATCHES * PATCH, left_col - PE_PATCHES * PATCH + wide)
                        dve.wait_ge(halo_ready, tile + 1)
                        at_borders = nc.vector.tensor_tensor(d[:, 0:PATCH:PATCH - 1, 0:wide],
                                                             rows[:, 1:PATCH - 1:PATCH - 3, c],
                                                             halo_bank[:, :, h], ALU.add)
                        if w == PE_PATCHES:
                            at_borders.then_inc(halo_free, 1)
                        nc.vector.tensor_tensor(d[:, 1:PATCH - 1, 0:wide], rows[:, 2:PATCH, c],
                                                rows[:, 0:PATCH - 2, c], ALU.subtract).then_inc(diff_ready, 1)

            def keep_record(tile, r, t):
                dve.wait_ge(analysed, tile + 1)
                nc.vector.tensor_scalar(records[:, bass.ds(t, 1), 0:3].rearrange("p a k -> p (a k)"),
                                        record[r][:], 1.0, None, ALU.mult)
                nc.vector.tensor_reduce(records[:, bass.ds(t, 1), 3:REC].rearrange("p a k -> p (a k)"),
                                        sums[r][:].rearrange("p k w -> p w k"), AX.X, ALU.add)\
                    .then_inc(recorded, 1)

            def fetch_coefficients(t):
                nc.vector.tensor_scalar(coef_now[:].rearrange("p a w -> p (a w)"),
                                        coef[:, bass.ds(t, 1)].rearrange("p t a w -> p (t a w)"),
                                        1.0, None, ALU.mult)

            def apply(pixels, signal):
                rows = pixels.rearrange("p (r w) -> p r w", w=WIDTH)
                for w in range(COLS):
                    v = rows[:, :, w * PATCH:(w + 1) * PATCH]
                    done = nc.vector.tensor_scalar(v, v, coef_now[:, 0, w:w + 1], coef_now[:, 1, w:w + 1],
                                                   ALU.mult, ALU.add)
                done.then_inc(signal, 1)

            def apply_again(image, g, w):
                dve.wait_ge(again_loaded[w % SLOTS],
                            16 * (2 * LOOPED * image - 2 * LOOPED + 2 * g + w // SLOTS + 1))
                apply(again[w % SLOTS][:], applied)

            def own_sums(r, items):
                for item in range(ITEMS - items, ITEMS):
                    slot, which, columns = DIFF_ITEMS[item]
                    wide = len(columns) * PATCH
                    nc.vector.tensor_reduce(sums[r][:, which, columns[0]:columns[-1] + 1],
                                            diff[slot][:, :, 0:wide]
                                            .rearrange("p r (w c) -> p w r c", w=len(columns)), AX.XY, ALU.add,
                                            apply_absolute_value=True)

            def output_half(image, g, w):
                if w % 2 == 0:
                    settle()
                    fetch_coefficients(RING * g + w // 2)
                    settle()
                apply_again(image, g, w)

            def step(image, g, u, before, after, count, output):
                tile = TILES * image + RING * g + u
                place = RING if u == RING else u
                early = EARLY_ITEMS if isinstance(g, int) and g == 0 and u == 0 else 0
                at_start, in_middle, at_end = output
                for w in at_start:
                    output_half(image, g, w)
                if not early:
                    settle()
                differences(tile, places[place], place, range(early, ITEMS))
                if before is not None:
                    keep_record(tile - 1, before, RING * g + u - 1)
                if place == RING:
                    nc.vector.tensor_scalar(records[:, LAST, 0:3], record[RING][:], 1.0, None, ALU.mult)
                    partition_spread()
                own = (OWN_SUMS_LAST if place == RING else
                       OWN_SUMS_FIRST if isinstance(image, int) and image == 0 else OWN_SUMS)
                if own:
                    settle()
                    own_sums(place, own)
                for w in in_middle:
                    output_half(image, g, w)
                if after is not None:
                    statistics(tile + 1, places[after], after, place_loaded[after], count)
                if place == RING:
                    stable_variance(image)
                for w in at_end:
                    output_half(image, g, w)
                if after is not None:
                    minus_mean(tile + 1, after)
                if place == RING:
                    score_most(image)

            def image_tiles(image, plan=None):
                last = isinstance(image, int) and image == IMAGES - 1
                nothing = [[[], [], []]] * (RING + 1)
                outputs = plan or (nothing, nothing, nothing)
                loads = [LOOPED * image - (b == 0) for b in range(RING)]
                step(image, 0, 0, None, 1, loads[1] + 1, outputs[0][0])
                step(image, 0, 1, 0, 2, loads[2] + 1, outputs[0][1])
                step(image, 0, 2, 1, 0, loads[0] + 2, outputs[0][2])
                with dve.Fori(1, LOOPED - 1) as g:
                    for u in range(RING):
                        b = (u + 1) % RING
                        step(image, g, u, (u - 1) % RING, b, loads[b] + g + (u + 1) // RING + 1, outputs[1][u])
                step(image, LOOPED - 1, 0, RING - 1, 1, loads[1] + LOOPED, outputs[2][0])
                step(image, LOOPED - 1, 1, 0, 2, loads[2] + LOOPED, outputs[2][1])
                step(image, LOOPED - 1, 2, 1, RING, image + 1, outputs[2][2])
                step(image, LOOPED - 1, RING, RING - 1, None if last else 0, LOOPED * image + LOOPED, outputs[2][3])

            part_mean, part_var, nm = (records[:, :, k] for k in range(3))

            def partition_spread():
                settle()
                nc.vector.tensor_tensor(spread2[:], part_mean, nm, ALU.add)
                settle()
                nc.vector.tensor_tensor(newton[:], spread2[:], spread2[:], ALU.mult)
                settle()
                nc.vector.tensor_tensor(spread[:], newton[:], part_var, ALU.add).then_inc(spread_ready, 1)

            def stable_variance(image):
                dve.wait_ge(var_ready, image + 1)
                nc.vector.tensor_scalar(var[:], var_bank, EPS, None, ALU.add).then_inc(stable_var_ready, 1)

            def score(sums_part, tiles, n):
                scale3 = scale[:, tiles].unsqueeze(2).broadcast_to([PARTS, n, COLS])
                nc.vector.tensor_tensor(scores[:, tiles], sums_part, scale3, ALU.mult)
                settle()
                nc.vector.tensor_tensor(by_band[:, tiles],
                                        scores[:, tiles].unsqueeze(2).broadcast_to([PARTS, n, BANDS, COLS]),
                                        same_band[:].unsqueeze(1).unsqueeze(3)
                                        .broadcast_to([PARTS, n, BANDS, COLS]),
                                        ALU.mult).then_inc(by_band_ready, 1)

            def score_most(image):
                dve.wait_ge(rstd_ready, image + 1)
                nc.vector.tensor_tensor(newton[:], rstd[:], rstd[:], ALU.mult)
                settle()
                nc.vector.tensor_tensor(spread2[:], newton[:], var[:], ALU.mult)
                settle()
                nc.vector.tensor_scalar(newton[:], spread2[:], -0.5, 1.5, ALU.mult, ALU.add)
                settle()
                nc.vector.tensor_tensor(scale[:], rstd[:], newton[:], ALU.mult)
                settle()
                score(records[:, 0:LAST, 3:REC], slice(0, LAST), LAST)

            def rank(image, output=(), last=False):
                dve.wait_ge(analysed, TILES * image + LAST + 1)
                nc.vector.tensor_reduce(records[:, LAST, 3:REC], sums[RING][:].rearrange("p k w -> p w k"),
                                        AX.X, ALU.add).then_inc(recorded, 1)
                settle()
                score(records[:, LAST:TILES, 3:REC], slice(LAST, TILES), 1)
                scale3 = scale[:].unsqueeze(2).broadcast_to([PARTS, TILES, COLS])
                if not last:
                    differences(TILES * image + TILES, ring[0], 0, range(EARLY_ITEMS))
                for w in output:
                    output_half(image, LOOPED - 1, w)
                dve.wait_ge(gathered, 2 * image + 2)
                nc.vector.tensor_copy(left, score_bank[0:PATCHES, :])
                settle()
                with dve.Fori(0, ROUNDS // ROUNDS_UNROLLED):
                    for _ in range(ROUNDS_UNROLLED):
                        nc.vector.max(largest[:], left)
                        settle()
                        nc.vector.match_replace(out=left, in_to_replace=largest[:], in_values=left,
                                                imm_value=-1.0)
                        settle()
                nc.vector.scalar_tensor_tensor(out=chosen,
                                               in0=left.unsqueeze(2).broadcast_to([PATCHES, CHANNELS, BANDS]),
                                               scalar=0.0,
                                               in1=same_channel[0:PATCHES, 0:BANDS].unsqueeze(1)
                                               .broadcast_to([PATCHES, CHANNELS, BANDS]),
                                               op0=ALU.is_lt, op1=ALU.mult).then_inc(chosen_ready, 1)
                dve.wait_ge(mask_ready, image + 1)
                nc.vector.tensor_tensor(scores[:],
                                        mask_bank.rearrange("p (t w) -> p t w", w=COLS),
                                        scale3, ALU.mult)
                settle()
                nc.vector.tensor_scalar(coef[:, :, 0, :], scores[:], 1.0, None, ALU.add)
                nc.vector.tensor_tensor(coef[:, :, 1, :], scores[:],
                                        nm.unsqueeze(2).broadcast_to([PARTS, TILES, COLS]), ALU.mult)
                settle()

            places = [*ring, kept]
            place_loaded = [*ring_loaded, kept_loaded]

            statistics(0, ring[0], 0, first_loaded, 1)
            minus_mean(0, 0)
            settle()
            differences(0, ring[0], 0, range(EARLY_ITEMS))
            dve.wait_ge(constants, CONSTANTS)
            nc.vector.tensor_reduce(same_band[:], plus[:].rearrange("p (c b) -> p b c", b=BANDS), AX.X, ALU.add)
            settle()
            nc.vector.tensor_copy(same_band16[:], same_band[:])
            image_tiles(0)

            def finish_kept():
                fetch_coefficients(LAST)
                settle()
                apply(kept[:, 0:HALF], applied)
                apply(kept[:, HALF:PIX], applied)

            plan = output_plan(OUTPUT)
            rank(0)
            finish_kept()
            with dve.Fori(1, IMAGES - 1) as image:
                image_tiles(image, plan)
                rank(image, plan[3])
                finish_kept()
            plan = output_plan(OUTPUT_OF_LAST)
            image_tiles(IMAGES - 1, plan)
            rank(IMAGES - 1, plan[3], True)

            for n, t in enumerate(order):
                settle()
                fetch_coefficients(t)
                settle()
                if n == 0:
                    apply(kept[:, 0:HALF], applied)
                    apply(kept[:, HALF:PIX], finished)
                else:
                    apply(buffers[n][:], finished)

            def finish(tile, pixels, loaded, count):
                settle()
                fetch_coefficients(tile)
                settle()
                dve.wait_ge(loaded, 16 * count)
                apply(pixels, finished)

            loads = 2 * LOOPED * (IMAGES - 1)
            for q in range(SLOTS):
                finish(q // 2, again[q][:], again_loaded[q], loads + 1)
            with dve.Fori(0, REFILLS // BUFFERS) as k:
                for b in range(BUFFERS):
                    finish(BUFFERS * k + b + 2, buffers[b][:], refilled[b], k + 1)
            for n in range(REFILLS // BUFFERS * BUFFERS, REFILLS):
                finish(n + 2, buffers[n % BUFFERS][:], refilled[n % BUFFERS], n // BUFFERS + 1)
            finish(SLOTS // 2, again[0][:], again_loaded[0], loads + 2)


def kernel(**inputs):
    import numpy as _np
    import concourse.bacc as _bacc
    from concourse import mybir as _mybir
    from concourse.bass_utils import run_bass_kernel_spmd as _run

    nc = _bacc.Bacc("TRN2", target_bir_lowering=False, num_devices=1)
    a = _np.ascontiguousarray(inputs["x"])
    shape = a.shape
    a = a.reshape(IMAGES * TILES, PARTS, PIX)
    x = nc.dram_tensor("in_x_dram", a.shape, _mybir.dt.from_np(a.dtype), kind="ExternalInput").ap()
    out = nc.dram_tensor("out_0_dram", a.shape, _mybir.dt.from_np(a.dtype), kind="ExternalOutput").ap()
    groupnorm_patch_topk(nc, x, out)
    r = _run(nc, [{"in_x_dram": a}], core_ids=[0])
    return r.results[0]["out_0_dram"].reshape(shape)
```
